# Optimizing a Trainium2 kernel written in Bass

```python
import numpy as np
import jax
import jax.numpy as jnp

def _softmax(x, axis=-1):
    return jax.nn.softmax(x, axis=axis)

def _gelu(x):
    return jax.nn.gelu(x, approximate=True)

def _silu(x):
    return jax.nn.silu(x)

def _sigmoid(x):
    return jax.nn.sigmoid(x)

def _layernorm(x, axis=-1, eps=1e-05):
    m = jnp.mean(x, axis=axis, keepdims=True)
    v = jnp.var(x, axis=axis, keepdims=True)
    return (x - m) / jnp.sqrt(v + eps)

def _scatter_add(tgt, idx, src, axis=0):
    return tgt.at[idx].add(src)

def _segment_sum(src, seg, n):
    return jax.ops.segment_sum(src, seg, n)
kernel_name = 'mk_recurrent_d2_jaxref_r8_68408b'

def setup_inputs(seed: int=0):
    np.random.seed(seed)
    _w = jnp.asarray

    def _L0_attn_setup():
        import jax, jax.numpy as jnp
        import numpy as np
        B, S, D_IN = (2, 256, 128)
        H, D_HEAD = (16, 64)
        key = jax.random.key(seed)
        k1, k2, k3 = jax.random.split(key, 3)
        x = jax.random.normal(k1, (B, S, D_IN), dtype=jnp.float32)
        kernel = jax.random.normal(k2, (3, H, D_IN, D_HEAD), dtype=jnp.float32) * np.float32(np.sqrt(2.0 / D_IN))
        WO = jax.random.normal(k3, (1, H * D_HEAD, D_IN), dtype=jnp.float32) * np.float32(np.sqrt(2.0 / (H * D_HEAD)))
        return {'x': x, 'kernel': kernel, 'WO': WO}
    _L0_attn_in = _L0_attn_setup()

    def _L0_ffn_setup():
        import jax, jax.numpy as jnp
        import numpy as np
        EMB = 128
        FF = 4 * EMB

        def _ternary(w):
            scale = jnp.maximum(jnp.mean(jnp.abs(w)), 1e-08)
            w_t = jnp.clip(jnp.round(w / scale), -1.0, 1.0)
            return w + jax.lax.stop_gradient(w_t - w)
        key = jax.random.key(seed)
        kx, k1, k2, kb1, kb2 = jax.random.split(key, 5)
        x = jax.random.normal(kx, (4, 256, EMB), dtype=jnp.float32)
        lim1 = 1.0 / np.sqrt(EMB)
        lim2 = 1.0 / np.sqrt(FF)
        W1 = jax.random.uniform(k1, (FF, EMB), jnp.float32, -lim1, lim1)
        b1 = jax.random.uniform(kb1, (FF,), jnp.float32, -lim1, lim1)
        W2 = jax.random.uniform(k2, (EMB, FF), jnp.float32, -lim2, lim2)
        b2 = jax.random.uniform(kb2, (EMB,), jnp.float32, -lim2, lim2)
        return {'x': x, 'W1': W1, 'b1': b1, 'W2': W2, 'b2': b2}
    _L0_ffn_in = _L0_ffn_setup()

    def _L1_attn_setup():
        import jax, jax.numpy as jnp
        import numpy as np
        B, S, D_MODEL, H, D = (2, 256, 128, 16, 64)
        SCALE = 1.0 / float(np.sqrt(D))

        def _rope(t, c, s):
            d2 = t.shape[-1] // 2
            t1, t2 = (t[..., :d2], t[..., d2:])
            return jnp.concatenate([t1 * c - t2 * s, t1 * s + t2 * c], axis=-1)
        key = jax.random.key(seed)
        ks = jax.random.split(key, 5)
        x = jax.random.normal(ks[0], (B, S, D_MODEL), jnp.float32)
        qkv_w = jax.random.normal(ks[1], (3 * H * D, D_MODEL), jnp.float32) * 0.02
        out_w = jax.random.normal(ks[2], (D_MODEL, H * D), jnp.float32) * 0.02
        bias_p = jax.random.uniform(ks[3], (H, 1, 1), jnp.float32) * 2.0
        bias_a = jax.random.uniform(ks[4], (H, 1, 1), jnp.float32)
        rope_freqs = 10000.0 ** (-jnp.arange(D // 2, dtype=jnp.float32) / (D // 2))
        return {'x': x, 'qkv_w': qkv_w, 'out_w': out_w, 'bias_p': bias_p, 'bias_a': bias_a, 'rope_freqs': rope_freqs}
    _L1_attn_in = _L1_attn_setup()

    def _L1_ffn_setup():
        import jax, jax.numpy as jnp
        import numpy as np
        B, S, D, F, E = (4, 256, 128, 512, 8)
        LN_EPS = 1e-05
        key = jax.random.key(seed)
        ks = jax.random.split(key, 6)
        sc = 0.02
        return {'x': jax.random.normal(ks[0], (B, S, D), dtype=jnp.float32), 'Wr': jax.random.normal(ks[1], (D, E), dtype=jnp.float32) * sc, 'br': jnp.zeros((E,), jnp.float32), 'ln_g': jnp.ones((D,), jnp.float32), 'ln_b': jnp.zeros((D,), jnp.float32), 'W1': jax.random.normal(ks[2], (E, D, F), dtype=jnp.float32) * sc, 'b1': jnp.zeros((E, F), jnp.float32), 'W2': jax.random.normal(ks[3], (E, F, D), dtype=jnp.float32) * sc, 'b2': jnp.zeros((E, D), jnp.float32)}
    _L1_ffn_in = _L1_ffn_setup()
    _d = {'L0_attn_x': _L0_attn_in['x'], 'L0_attn_kernel': _L0_attn_in['kernel'], 'L0_attn_WO': _L0_attn_in['WO'], 'L0_ffn_W1': _L0_ffn_in['W1'], 'L0_ffn_b1': _L0_ffn_in['b1'], 'L0_ffn_W2': _L0_ffn_in['W2'], 'L0_ffn_b2': _L0_ffn_in['b2'], 'L1_attn_qkv_w': _L1_attn_in['qkv_w'], 'L1_attn_out_w': _L1_attn_in['out_w'], 'L1_attn_bias_p': _L1_attn_in['bias_p'], 'L1_attn_bias_a': _L1_attn_in['bias_a'], 'L1_attn_rope_freqs': _L1_attn_in['rope_freqs'], 'L1_ffn_Wr': _L1_ffn_in['Wr'], 'L1_ffn_br': _L1_ffn_in['br'], 'L1_ffn_ln_g': _L1_ffn_in['ln_g'], 'L1_ffn_ln_b': _L1_ffn_in['ln_b'], 'L1_ffn_W1': _L1_ffn_in['W1'], 'L1_ffn_b1': _L1_ffn_in['b1'], 'L1_ffn_W2': _L1_ffn_in['W2'], 'L1_ffn_b2': _L1_ffn_in['b2']}
    _x0 = _d['L0_attn_x']
    _d['L0_attn_x'] = jax.random.normal(jax.random.fold_in(jax.random.key(seed), 1), (1, 2048, 128), dtype=_x0.dtype)
    del _x0
    return _d

def reference(L0_attn_x, L0_attn_kernel, L0_attn_WO, L0_ffn_W1, L0_ffn_b1, L0_ffn_W2, L0_ffn_b2, L1_attn_qkv_w, L1_attn_out_w, L1_attn_bias_p, L1_attn_bias_a, L1_attn_rope_freqs, L1_ffn_Wr, L1_ffn_br, L1_ffn_ln_g, L1_ffn_ln_b, L1_ffn_W1, L1_ffn_b1, L1_ffn_W2, L1_ffn_b2):

    def _L0_attn_ref(x, kernel, WO):
        import jax, jax.numpy as jnp
        import numpy as np
        B, S, D_IN = (2, 256, 128)
        H, D_HEAD = (16, 64)
        b, s, _ = x.shape
        h, d = (kernel.shape[1], kernel.shape[3])
        q = jnp.einsum('bsm,hmd->bhsd', x, kernel[0])
        k = jnp.einsum('bsm,hmd->bhsd', x, kernel[1])
        v = jnp.einsum('bsm,hmd->bhsd', x, kernel[2])
        scale = jnp.float32(1.0 / (d * d * h))
        scores = jnp.einsum('bhsd,bhtd->bhst', q, k) * scale
        attn = jax.nn.softmax(scores, axis=-1)
        out = jnp.einsum('bhst,bhtd->bhsd', attn, v)
        out = jnp.transpose(out, (0, 2, 3, 1)).reshape(b, s, d * h)
        out = jnp.einsum('bsf,fm->bsm', out, WO[0])
        return out

    def _L0_ffn_ref(x, W1, b1, W2, b2):
        import jax, jax.numpy as jnp
        import numpy as np
        EMB = 128
        FF = 4 * EMB

        def _ternary(w):
            scale = jnp.maximum(jnp.mean(jnp.abs(w)), 1e-08)
            w_t = jnp.clip(jnp.round(w / scale), -1.0, 1.0)
            return w + jax.lax.stop_gradient(w_t - w)
        h = jnp.einsum('bsd,fd->bsf', x, _ternary(W1)) + b1
        h = jax.nn.gelu(h, approximate=False)
        out = jnp.einsum('bsf,df->bsd', h, _ternary(W2)) + b2
        return out

    def _L1_attn_ref(x, qkv_w, out_w, bias_p, bias_a, rope_freqs):
        import jax, jax.numpy as jnp
        import numpy as np
        B, S, D_MODEL, H, D = (2, 256, 128, 16, 64)
        SCALE = 1.0 / float(np.sqrt(D))

        def _rope(t, c, s):
            d2 = t.shape[-1] // 2
            t1, t2 = (t[..., :d2], t[..., d2:])
            return jnp.concatenate([t1 * c - t2 * s, t1 * s + t2 * c], axis=-1)
        Bb, Ss, _ = x.shape
        qkv = (x @ qkv_w.T).reshape(Bb, Ss, 3, H, D)
        q = qkv[:, :, 0].transpose(0, 2, 1, 3)
        k = qkv[:, :, 1].transpose(0, 2, 1, 3)
        v = qkv[:, :, 2].transpose(0, 2, 1, 3)
        pos = jnp.arange(Ss, dtype=jnp.float32)
        ang = pos[:, None] * rope_freqs[None, :]
        c = jnp.cos(ang)[None, None]
        s = jnp.sin(ang)[None, None]
        q = _rope(q, c, s)
        k = _rope(k, c, s)
        scores = jnp.einsum('bhqd,bhkd->bhqk', q, k) * SCALE
        p = jnp.maximum(bias_p, 0.01)
        a = jnp.maximum(bias_a, 0.01)
        dist = jnp.abs(pos[None, :] - pos[:, None])
        kb = -p * jnp.log1p(a * dist)
        attn = jax.nn.softmax(scores + kb[None], axis=-1)
        out = jnp.einsum('bhqk,bhkd->bhqd', attn, v)
        out = out.transpose(0, 2, 1, 3).reshape(Bb, Ss, H * D)
        return out @ out_w.T

    def _L1_ffn_ref(x, Wr, br, ln_g, ln_b, W1, b1, W2, b2):
        import jax, jax.numpy as jnp
        import numpy as np
        B, S, D, F, E = (4, 256, 128, 512, 8)
        LN_EPS = 1e-05
        tokens_shape = x.shape[:-1]
        xt = x.reshape(-1, x.shape[-1])
        router_logits = xt @ Wr + br
        router_probs = jax.nn.softmax(router_logits, axis=-1)
        gates = jnp.max(router_probs, axis=-1, keepdims=True)
        idx = jnp.argmax(router_probs, axis=-1)
        onehot = jax.nn.one_hot(idx, E, dtype=xt.dtype)
        mu = jnp.mean(xt, axis=-1, keepdims=True)
        var = jnp.mean(jnp.square(xt - mu), axis=-1, keepdims=True)
        xn = (xt - mu) * jax.lax.rsqrt(var + LN_EPS) * ln_g + ln_b
        h = jnp.einsum('te,td,edf->tf', onehot, xn, W1) + b1[idx]
        h = jax.nn.relu(h)
        y = jnp.einsum('te,tf,efd->td', onehot, h, W2) + b2[idx]
        y = y * gates
        return y.reshape(tokens_shape + (y.shape[-1],))
    x = L0_attn_x
    xn = _layernorm(x, axis=-1)
    s = _L0_attn_ref(xn, L0_attn_kernel, L0_attn_WO)
    g = _silu(_L0_ffn_ref(xn, L0_ffn_W1, L0_ffn_b1, L0_ffn_W2, L0_ffn_b2))
    x = x + s * g
    xn = _layernorm(x, axis=-1)
    s = _L1_attn_ref(xn, L1_attn_qkv_w, L1_attn_out_w, L1_attn_bias_p, L1_attn_bias_a, L1_attn_rope_freqs)
    g = _silu(_L1_ffn_ref(xn, L1_ffn_Wr, L1_ffn_br, L1_ffn_ln_g, L1_ffn_ln_b, L1_ffn_W1, L1_ffn_b1, L1_ffn_W2, L1_ffn_b2))
    x = x + s * g
    return x

_drawn_inputs = setup_inputs


def setup_inputs(seed=0):
    import zlib

    import numpy as np

    out = dict(_drawn_inputs(seed))
    spreads = {'L1_ffn_br': (0.0, 0.8),
     'L1_ffn_ln_g': (1.0, 0.6),
     'L1_ffn_ln_b': (0.0, 0.8),
     'L1_ffn_b1': (0.0, 0.8),
     'L1_ffn_b2': (0.0, 0.8)}
    factors = {'L0_ffn_b1': 8.0,
     'L0_ffn_b2': 8.0,
     'L1_attn_qkv_w': 8.0,
     'L1_attn_out_w': 8.0,
     'L1_attn_bias_p': 8.0,
     'L1_attn_bias_a': 8.0,
     'L1_attn_rope_freqs': 8.0,
     'L1_ffn_Wr': 8.0,
     'L1_ffn_W1': 8.0,
     'L1_ffn_W2': 8.0}
    for name, (base, spread) in spreads.items():
        noise = np.random.default_rng([zlib.crc32(name.encode()), seed]).standard_normal(out[name].shape)
        drawn = base * np.exp(spread * noise) if base else spread * noise
        out[name] = jnp.asarray(drawn.astype(out[name].dtype))
    for name, factor in factors.items():
        out[name] = (out[name] * factor).astype(out[name].dtype)
    return out
```

```python
import concourse.bass as bass
from concourse import mybir
from contextlib import ExitStack

F32 = mybir.dt.float32
F16 = mybir.dt.float16
BF16 = mybir.dt.bfloat16
ALU = mybir.AluOpType
ACT = mybir.ActivationFunctionType
AX = mybir.AxisListType

P = 128
D = 128
S = 2048
H = 16
DH = 64
NT = S // P
QC = 512
NC = S // QC
NCH = H * NC
KP = 2
NS = NT // KP
FF = 512
FT = FF // P
NE = 8
LN_EPS = 1e-05
TINY = 1e-30
MAXROW = P
RING = 4
LAG = 2
ROUND = 12582912.0
LINE = 2 * S
BW = S - P + S - QC + QC
AHEAD = 2
NJ = 16
ROW_STEP, OUT_STEPS = 1, (3, 4)
POOL_STEPS = (0, 1, 5)
POOL_RANK = {s: i for i, s in enumerate(POOL_STEPS)}
VEC_STEPS = tuple(s for s in range(NS) if s not in POOL_STEPS)
VEC_RANK = {s: i for i, s in enumerate(VEC_STEPS)}
LOADS = 6


class Memory:

    def __init__(self, nc, ctx):
        self.nc, self.ctx = nc, ctx

    def sb(self, name, shape, dt=F32):
        return self.ctx.enter_context(self.nc.sbuf_tensor(name, shape, dt))

    def ps(self, name, shape, dt=F32):
        return self.ctx.enter_context(self.nc.psum_tensor(name, shape, dt))

    def sem(self, name):
        return self.ctx.enter_context(self.nc.semaphore(name))


def is_zero(n):
    return isinstance(n, int) and n == 0


def apart(eng, sem):
    eng.wait_ge(sem, 1)


def flat(ap):
    return ap.rearrange("p a b -> p (a b)")


def constants_stage(nc, k, x):
    with ExitStack() as ctx:
        m = Memory(nc, ctx)
        zeroed, made, loaded = m.sem("c_zeroed"), m.sem("c_made"), m.sem("c_loaded")
        block = ctx.enter_context(nc.Block())

        @block.sync
        def _(sp):
            sp.dma_start(k.x[:, :, :], x.rearrange("a (t p) m -> p (a t) m", p=P)).then_inc(loaded, 16)
            sp.wait_ge(loaded, 16)

        @block.gpsimd
        def _(pool):
            nc.gpsimd.memset(k.ident[:, :], 0.0).then_inc(zeroed, 1)
            nc.gpsimd.memset(k.flip[:, :], 0.0).then_inc(zeroed, 1)
            nc.gpsimd.memset(k.ones[:, :], 1.0)
            nc.gpsimd.memset(k.ones32[:, :], 1.0 / 32)
            pool.wait_ge(zeroed, 2)
            nc.gpsimd.affine_select(out=k.ident[:, :], in_=k.ident[:, :], compare_op=ALU.not_equal, fill=1.0,
                                    base=0, pattern=[[-1, P]], channel_multiplier=1)
            nc.gpsimd.affine_select(out=k.flip[:, :], in_=k.flip[:, :], compare_op=ALU.not_equal, fill=1.0,
                                    base=-(P - 1), pattern=[[1, P]], channel_multiplier=1)


def layernorm_stage(nc, k, tag, src, dst, dstT, affine=None):
    with ExitStack() as ctx:
        m = Memory(nc, ctx)
        stats, mv = m.sb(tag + "stats", [P, NT, 6]), m.sb(tag + "mv", [P, NT, 2])
        std, rstd = m.sb(tag + "std", [P, NT]), m.sb(tag + "rstd", [P, NT])
        tp = m.ps(tag + "tp", [P, 4, 4, P])
        stats_done, mv_done, var_done = m.sem(tag + "stats_done"), m.sem(tag + "mv_done"), m.sem(tag + "var_done")
        std_done, rstd_done, tile_done = m.sem(tag + "std_done"), m.sem(tag + "rstd_done"), m.sem(tag + "tile_done")
        turned, copied, scaled = m.sem(tag + "turned"), m.sem(tag + "copied"), m.sem(tag + "scaled")
        block = ctx.enter_context(nc.Block())

        @block.vector
        def _(ve):
            for t in range(NT):
                nc.vector.bn_stats(stats[:, t, :], src[:, t, :]).then_inc(stats_done, 1)
            for t in range(NT):
                ve.wait_ge(stats_done, t + 1)
                nc.vector.bn_aggr(mv[:, t, :], stats[:, t, :]).then_inc(mv_done, 1)
            ve.wait_ge(mv_done, NT)
            nc.vector.tensor_scalar(std[:, :], mv[:, :, 1], LN_EPS, None, ALU.add).then_inc(var_done, 1)
            ve.wait_ge(std_done, 1)
            nc.vector.reciprocal(rstd[:, :], std[:, :]).then_inc(rstd_done, 1)
            ve.wait_ge(rstd_done, 1)
            for t in range(NT):
                ins = nc.vector.tensor_scalar(dst[:, t, :], src[:, t, :], mv[:, t, 0:1], rstd[:, t:t + 1],
                                              ALU.subtract, ALU.mult)
                if affine is None:
                    ins.then_inc(tile_done, 1)
                else:
                    gain, shift = affine
                    ins.then_inc(scaled, 1)
                    ve.wait_ge(scaled, 2 * t + 1)
                    nc.vector.tensor_tensor(dst[:, t, :], dst[:, t, :], gain, ALU.mult).then_inc(scaled, 1)
                    ve.wait_ge(scaled, 2 * t + 2)
                    nc.vector.tensor_tensor(dst[:, t, :], dst[:, t, :], shift, ALU.add).then_inc(tile_done, 1)

        @block.tensor
        def _(pe):
            for t in range(NT):
                pe.wait_ge(tile_done, t + 1)
                nc.tensor.transpose(tp[:, t // 4, t % 4, :], dst[:, t, :], k.ident[:, :]).then_inc(turned, 1)

        @block.scalar
        def _(act):
            act.wait_ge(var_done, 1)
            nc.scalar.activation(std[:, :], std[:, :], ACT.Sqrt).then_inc(std_done, 1)
            for g in range(4):
                act.wait_ge(turned, 4 * g + 4)
                nc.scalar.activation(dstT[:, 4 * g * P:4 * (g + 1) * P], flat(tp[:, g, :, :]), ACT.Copy)\
                   .then_inc(copied, 1)


def ternary_ffn_stage(nc, k, W1, b1, W2, b2, gate):
    with ExitStack() as ctx:
        m = Memory(nc, ctx)
        w = m.sb("tf_w", [P, 2, FF])
        mag = m.sb("tf_mag", [P, 2, FF])
        part, scale = m.sb("tf_part", [P, 2]), m.sb("tf_scale", [P, 2])
        above, below = m.sb("tf_above", [P, 2]), m.sb("tf_below", [P, 2])
        t = m.sb("tf_t", [P, 2, FF])
        wT = m.sb("tf_wT", [P, 2, FF])
        bias1, bias2 = m.sb("tf_b1", [P, FT]), m.sb("tf_b2", [1, D])
        hT = m.sb("tf_hT", [P, FT, S])
        ps = m.ps("tf_ps", [P, 8, 512])
        loaded, mags, summed, scaled = m.sem("tf_loaded"), m.sem("tf_mags"), m.sem("tf_summed"), m.sem("tf_scaled")
        chain, turned, copied = m.sem("tf_chain"), m.sem("tf_turned"), m.sem("tf_copied")
        up, act_done, down, gated = m.sem("tf_up"), m.sem("tf_act"), m.sem("tf_down"), m.sem("tf_gated")
        block = ctx.enter_context(nc.Block())

        @block.sync
        def _(sp):
            sp.dma_start(w[:, 0, :].rearrange("p (j m) -> p j m", m=D),
                         W1.rearrange("(j p) m -> p j m", p=P)).then_inc(loaded, 16)
            sp.dma_start(w[:, 1, :], W2).then_inc(loaded, 16)
            sp.dma_start(bias1[:, :], b1.rearrange("(j p) -> p j", p=P),
                         allow_slow_non_contiguous=True).then_inc(loaded, 16)
            sp.dma_start(bias2[:, :], b2.rearrange("(a d) -> a d", a=1)).then_inc(loaded, 16)

        @block.scalar
        def _(act):
            act.wait_ge(loaded, 64)
            for i in range(2):
                nc.scalar.activation(mag[:, i, :], w[:, i, :], ACT.Abs).then_inc(mags, 1)
            for i in range(2):
                act.wait_ge(turned, i + 1)
                nc.scalar.activation(wT[:, i, :], ps[:, 1 + i, :], ACT.Copy).then_inc(copied, 1)
            for j in range(FT):
                for c in range(NC):
                    n = NC * j + c
                    act.wait_ge(up, n + 1)
                    nc.scalar.activation(hT[:, j, c * QC:(c + 1) * QC], ps[:, n % 4, :], ACT.Gelu,
                                         bias=bias1[:, j:j + 1]).then_inc(act_done, 1)
            for g in range(NT // 4):
                act.wait_ge(down, g + 1)
                nc.scalar.activation(flat(gate[:, 4 * g:4 * g + 4, :]), ps[:, 4 + g, :], ACT.Silu).then_inc(gated, 1)

        @block.vector
        def _(ve):
            done = 0

            def link(ins):
                nonlocal done
                done += 1
                ins.then_inc(chain, 1)
                ve.wait_ge(chain, done)

            ve.wait_ge(mags, 2)
            for i in range(2):
                link(nc.vector.reduce_sum(part[:, i:i + 1], mag[:, i, :], AX.X))
            ve.wait_ge(summed, 1)
            link(nc.vector.tensor_scalar(scale[:, :], ps[:, 0, 0:2], 1.0 / (FF * D), 1e-08, ALU.mult, ALU.max))
            link(nc.vector.tensor_scalar(above[:, :], scale[:, :], 0.5, None, ALU.mult))
            link(nc.vector.tensor_scalar(below[:, :], scale[:, :], -0.5, None, ALU.mult))
            for i in range(2):
                link(nc.vector.tensor_scalar(t[:, i, :], w[:, i, :], below[:, i:i + 1], None, ALU.is_lt))
                link(nc.vector.scalar_tensor_tensor(t[:, i, :], w[:, i, :], above[:, i:i + 1], t[:, i, :],
                                                    ALU.is_gt, ALU.subtract))
                link(nc.vector.tensor_tensor(t[:, i, :], t[:, i, :], w[:, i, :], ALU.subtract))
                nc.vector.tensor_tensor(t[:, i, :], t[:, i, :], w[:, i, :], ALU.add).then_inc(scaled, 1)

        @block.tensor
        def _(pe):
            pe.wait_ge(chain, 2)
            nc.tensor.matmul(ps[:, 0, 0:2], k.ones[:, 0:P], part[:, :], start=True, stop=True).then_inc(summed, 1)
            for i in range(2):
                pe.wait_ge(scaled, i + 1)
                for j in range(FT):
                    last = nc.tensor.transpose(ps[:, 1 + i, j * P:(j + 1) * P], t[:, i, j * P:(j + 1) * P],
                                               k.ident[:, :])
                last.then_inc(turned, 1)
            pe.wait_ge(copied, 2)
            for j in range(FT):
                for c in range(NC):
                    n = NC * j + c
                    if n >= 4:
                        pe.wait_ge(act_done, n - 3)
                    nc.tensor.matmul(ps[:, n % 4, :], wT[:, 0, j * P:(j + 1) * P], k.xnT[:, c * QC:(c + 1) * QC],
                                     start=True, stop=True).then_inc(up, 1)
            pe.wait_ge(act_done, FT * NC)
            for q in range(NT):
                o = ps[:, 4 + q // 4, (q % 4) * P:(q % 4 + 1) * P]
                for j in range(FT):
                    nc.tensor.matmul(o, hT[:, j, q * P:(q + 1) * P], wT[:, 1, j * P:(j + 1) * P],
                                     start=(j == 0), stop=False)
                last = nc.tensor.matmul(o, k.ones[0:1, 0:P], bias2[:, :], start=False, stop=True)
                if q % 4 == 3:
                    last.then_inc(down, 1)


def peak_of_weights(nc, ve, link, w, n, hi, lo, amax):
    for i in range(n):
        link(nc.vector.reduce_max(hi[:, i:i + 1], w[:, i, :], AX.X))
        link(nc.vector.tensor_reduce(lo[:, i:i + 1], w[:, i, :], AX.X, ALU.min))
    link(nc.vector.scalar_tensor_tensor(amax[:, 0:n], lo[:, 0:n], -1.0, hi[:, 0:n], ALU.mult, ALU.max))


def load_weights_stage(nc, k, w, W, Wo):
    with ExitStack() as ctx:
        loaded = Memory(nc, ctx).sem("lw_loaded")
        block = ctx.enter_context(nc.Block())

        @block.sync
        def _(sp):
            for i in range(3):
                sp.dma_start(w[:, i, :].rearrange("p (h d) -> p h d", h=H),
                             W[i].rearrange("h m d -> m h d")).then_inc(loaded, 16)
            for half in range(2):
                sp.dma_start(k.wo[half * DH:(half + 1) * DH, :, :],
                             Wo[0].rearrange("(d h) m -> d h m", h=H)).then_inc(loaded, 16)
            sp.wait_ge(loaded, 80)


def turn_weights_stage(nc, k, w, Wqkv, Wo):
    with ExitStack() as ctx:
        m = Memory(nc, ctx)
        NW = 3 * H * DH // P
        raw = m.sb("tw_raw", [P, NW, D])
        out2 = m.sb("tw_out2", [P, H, 2, DH])
        ps = m.ps("tw_ps", [P, 8, 4, P])
        loaded, loaded_o, turned, copied = m.sem("tw_loaded"), m.sem("tw_loaded_o"), m.sem("tw_turned"), m.sem("tw_copied")
        NG = (NW + H) // 4
        block = ctx.enter_context(nc.Block())

        @block.sync
        def _(sp):
            sp.dma_start(raw[:, :, :], Wqkv.rearrange("(t p) m -> p t m", p=P)).then_inc(loaded, 16)
            for half in range(2):
                sp.dma_start(out2[:, :, half, :], Wo.rearrange("m (h d) -> m h d", h=H)).then_inc(loaded_o, 16)

        @block.tensor
        def _(pe):
            pe.wait_ge(loaded, 16)
            for g in range(NG):
                if g == NW // 4:
                    pe.wait_ge(loaded_o, 32)
                if g >= 8:
                    pe.wait_ge(copied, g - 7)
                for q in range(4):
                    t = 4 * g + q
                    src = raw[:, t, :] if t < NW else out2[:, t - NW, :, :].rearrange("p a d -> p (a d)")
                    last = nc.tensor.transpose(ps[:, g % 8, q, :], src, k.ident[:, :])
                last.then_inc(turned, 1)

        @block.scalar
        def _(act):
            for g in range(NG):
                act.wait_ge(turned, g + 1)
                n = 4 * g
                if n < NW:
                    i, at = n // 8, (n % 8) * P
                    dst = w[:, i, at:at + 4 * P]
                else:
                    dst = flat(k.wo[:, n - NW:n - NW + 4, :])
                nc.scalar.activation(dst, flat(ps[:, g % 8, :, :]), ACT.Copy).then_inc(copied, 1)


TWO_PI_PARTS = (6.28125, 2029.0 / 2**20, 2 * 3.141592653589793 - 6.28125 - 2029.0 / 2**20)
HALF_PI = 1.5707963267948966
PI_INSIDE = 3.1415925


def rope_stage(nc, k, table, freqs):
    with ExitStack() as ctx:
        m = Memory(nc, ctx)
        pos = m.sb("rp_pos", [P, S], mybir.dt.int32)
        ang, turns = m.sb("rp_ang", [P, S]), m.sb("rp_turns", [P, S])
        freq = m.sb("rp_freq", [P, 1])
        loaded, counted, chain, reduced, done_ = (m.sem("rp_loaded"), m.sem("rp_counted"), m.sem("rp_chain"),
                                                  m.sem("rp_reduced"), m.sem("rp_done"))
        block = ctx.enter_context(nc.Block())

        @block.sync
        def _(sp):
            for q in range(P // 32):
                sp.dma_start(freq[32 * q:32 * q + 32, :], freqs.rearrange("(d a) -> d a", a=1),
                             allow_slow_non_contiguous=True).then_inc(loaded, 16)

        @block.gpsimd
        def _(pool):
            nc.gpsimd.iota(pos[:, :], pattern=[[1, S]], base=0, channel_multiplier=0).then_inc(counted, 1)

        @block.vector
        def _(ve):
            done = 0

            def link(ins):
                nonlocal done
                done += 1
                ins.then_inc(chain, 1)
                ve.wait_ge(chain, done)

            ve.wait_ge(counted, 1)
            link(nc.vector.tensor_copy(ang[:, :], pos[:, :]))
            ve.wait_ge(loaded, 16 * (P // 32))
            link(nc.vector.tensor_scalar(ang[:, :], ang[:, :], freq[:, 0:1], None, ALU.mult))
            for i in range(2):
                quarter = 0.25 if i == 0 else 0.0
                r = table[:, i, :]
                link(nc.vector.tensor_scalar(turns[:, :], ang[:, :], 0.15915494309189535, quarter, ALU.mult, ALU.add))
                link(nc.vector.tensor_scalar(turns[:, :], turns[:, :], ROUND, ROUND, ALU.add, ALU.subtract))
                for j, part in enumerate(TWO_PI_PARTS):
                    link(nc.vector.scalar_tensor_tensor(r, turns[:, :], -part, ang[:, :] if j == 0 else r,
                                                        ALU.mult, ALU.add))
                if i == 0:
                    link(nc.vector.tensor_scalar(r, r, HALF_PI, None, ALU.add))
                nc.vector.tensor_scalar(r, r, PI_INSIDE, -PI_INSIDE, ALU.min, ALU.max).then_inc(reduced, 1)

        @block.scalar
        def _(act):
            for i in range(2):
                act.wait_ge(reduced, i + 1)
                nc.scalar.activation(table[:, i, :], table[:, i, :], ACT.Sin).then_inc(done_, 1)


def bias_stage(nc, k, bias_p, bias_a):
    LOW = -60000.0
    with ExitStack() as ctx:
        m = Memory(nc, ctx)
        ints = m.sb("bs_ints", [H, LINE], mybir.dt.int32)
        dist = m.sb("bs_dist", [H, LINE])
        hi, lo = m.sb("bs_hi", [H, LINE], F16), m.sb("bs_lo", [H, LINE], F16)
        p, a = m.sb("bs_p", [H, 1]), m.sb("bs_a", [H, 1])
        unit16, q = m.sb("bs_unit16", [P, 1], BF16), m.sb("bs_q", [P, 1])
        loaded, counted, chain, ready = m.sem("bs_loaded"), m.sem("bs_counted"), m.sem("bs_chain"), m.sem("bs_ready")
        logged, high, low, stored = m.sem("bs_logged"), m.sem("bs_high"), m.sem("bs_low"), m.sem("bs_stored")
        block = ctx.enter_context(nc.Block())

        @block.sync
        def _(sp):
            sp.dma_start(p[:, :], bias_p.rearrange("h a b -> h (a b)"),
                         allow_slow_non_contiguous=True).then_inc(loaded, 16)
            sp.dma_start(a[:, :], bias_a.rearrange("h a b -> h (a b)"),
                         allow_slow_non_contiguous=True).then_inc(loaded, 16)
            sp.wait_ge(high, 1)
            sp.dma_start(k.bias_line[0], hi[:, :]).then_inc(stored, 16)
            sp.wait_ge(low, 1)
            sp.dma_start(k.bias_line[1], lo[:, :]).then_inc(stored, 16)
            sp.wait_ge(stored, 32)

        @block.gpsimd
        def _(pool):
            nc.gpsimd.iota(ints[:, :], pattern=[[1, LINE]], base=-(S - 1), channel_multiplier=0).then_inc(counted, 1)

        @block.vector
        def _(ve):
            done = 0

            def link(ins):
                nonlocal done
                done += 1
                ins.then_inc(chain, 1)
                ve.wait_ge(chain, done)

            link(nc.vector.reciprocal(k.unit[:, :], k.sscale[:, :]))
            link(nc.vector.tensor_copy(unit16[:, :], k.unit[:, :]))
            link(nc.vector.tensor_copy(k.unit[:, :], unit16[:, :]))
            link(nc.vector.tensor_scalar(k.flipu[:, :], k.flip[:, :], k.unit[:, 0:1], None, ALU.mult))
            link(nc.vector.tensor_tensor(q[:, :], k.unit[:, :], k.sscale[:, :], ALU.mult))
            link(nc.vector.reciprocal(q[:, :], q[:, :]))
            ve.wait_ge(loaded, 32)
            link(nc.vector.tensor_scalar(a[:, :], a[:, :], 0.01, None, ALU.max))
            link(nc.vector.tensor_scalar(p[:, :], p[:, :], 0.01, -1.0, ALU.max, ALU.mult))
            link(nc.vector.tensor_tensor(p[:, :], p[:, :], q[0:H, :], ALU.mult))
            ve.wait_ge(counted, 1)
            link(nc.vector.tensor_copy(dist[:, :], ints[:, :]))
            nc.vector.tensor_scalar(q[:, :], q[:, :], 1.0, None, ALU.mult).then_inc(ready, 1)
            ve.wait_ge(logged, 2)
            link(nc.vector.tensor_scalar(dist[:, :], dist[:, :], p[:, 0:1], LOW, ALU.mult, ALU.max))
            nc.vector.tensor_copy(hi[:, :], dist[:, :]).then_inc(high, 1)
            ve.wait_ge(high, 1)
            nc.vector.tensor_tensor(lo[:, :], dist[:, :], hi[:, :], ALU.subtract).then_inc(low, 1)

        @block.scalar
        def _(act):
            act.wait_ge(ready, 1)
            nc.scalar.activation(dist[:, :], dist[:, :], ACT.Abs).then_inc(logged, 1)
            act.wait_ge(logged, 1)
            nc.scalar.activation(dist[:, :], dist[:, :], ACT.Ln, scale=a[:, 0:1], bias=k.ones[0:H, 0:1])\
               .then_inc(logged, 1)


def qkv_stage(nc, k, layer, w, softmax_scale, rope=None):
    rotate = rope is not None
    with ExitStack() as ctx:
        m = Memory(nc, ctx)
        g = f"q{layer}_"
        wsw = m.sb(g + "wsw", [P, 2, H * DH]) if rotate else None
        hi, lo = m.sb(g + "hi", [P, 3]), m.sb(g + "lo", [P, 3])
        amax, peak = m.sb(g + "amax", [P, 3]), m.sb(g + "peak", [3, 1])
        diag, inv = m.sb(g + "diag", [3, 3]), m.sb(g + "inv", [P, 3])
        bc = m.sb(g + "bc", [P, 3])
        NB = 4
        ps = m.ps(g + "ps", [P, NB, 1024])
        oh, ol = m.sb(g + "oh", [P, 2, S], F16), m.sb(g + "ol", [P, 2, S], F16)
        t1 = m.sb(g + "t1", [P, 2, 1024]) if rotate else None
        t2 = m.sb(g + "t2", [P, 2, 1024]) if rotate else None
        chain, turned, peaked = m.sem(g + "chain"), m.sem(g + "turned"), m.sem(g + "peaked")
        job, high, low, stored = m.sem(g + "job"), m.sem(g + "high"), m.sem(g + "low"), [m.sem(g + "stored0"), m.sem(g + "stored1")]
        wready, scaled = m.sem(g + "wready"), m.sem(g + "scaled")
        prod, rot = m.sem(g + "prod"), m.sem(g + "rot")
        NV = NT
        pairs = [(pr, i, half) for pr in range(H // 2) for i in range(2) for half in range(2)]
        block = ctx.enter_context(nc.Block())

        @block.sync
        def _(sp):
            for n in range(2 * (H // 2)):
                pr, i = divmod(n, 2)
                sp.wait_ge(high, NV + 2 * n + 2)
                sp.wait_ge(low, NV + 2 * n + 2)
                sp.dma_start(k.qk_high[i, pr], oh[:, n % 2, :]).then_inc(stored[n % 2], 16)
                sp.dma_start(k.qk_low[i, pr], ol[:, n % 2, :]).then_inc(stored[n % 2], 16)
            for b in range(2):
                sp.wait_ge(stored[b], 32 * (H // 2))

        @block.vector
        def _(ve):
            done = 0

            def link(ins):
                nonlocal done
                done += 1
                ins.then_inc(chain, 1)
                ve.wait_ge(chain, done)

            peak_of_weights(nc, ve, link, w, 3, hi, lo, amax)
            nc.vector.tensor_copy(bc[:, :], amax[:, :]).then_inc(scaled, 1)
            ve.wait_ge(turned, 1)
            link(nc.vector.reduce_max(peak[:, :], ps[0:3, 0, 0:P], AX.X))
            link(nc.vector.tensor_scalar(peak[:, :], peak[:, :], TINY, None, ALU.max))
            nc.vector.tensor_scalar(diag[:, :], k.ident[0:3, 0:3], peak[:, 0:1], None, ALU.mult).then_inc(scaled, 1)
            ve.wait_ge(peaked, 1)
            link(nc.vector.tensor_copy(bc[:, :], ps[:, 1, 0:3]))
            link(nc.vector.reciprocal(inv[:, :], bc[:, :]))
            link(nc.vector.tensor_tensor(k.sscale[:, 0:1], bc[:, 0:1], bc[:, 1:2], ALU.mult))
            link(nc.vector.tensor_scalar(k.sscale[:, 0:1], k.sscale[:, 0:1], softmax_scale, None, ALU.mult))
            for i in (2, 0, 1):
                nc.vector.tensor_scalar(w[:, i, :], w[:, i, :], inv[:, i:i + 1], None, ALU.mult).then_inc(wready, 1)
            if rotate:
                ve.wait_ge(wready, 3)
                wq = w[:, 0:2, :].rearrange("p i (h r d) -> p (i h) r d", h=H, r=2)
                wp = wsw[:, :, :].rearrange("p i (h r d) -> p (i h) r d", h=H, r=2)
                nc.vector.tensor_scalar(wp[:, :, 0, :], wq[:, :, 1, :], -1.0, None, ALU.mult).then_inc(wready, 1)
                nc.vector.tensor_copy(wp[:, :, 1, :], wq[:, :, 0, :]).then_inc(wready, 1)
            nc.vector.tensor_scalar(flat(k.wo[:, :, :]), flat(k.wo[:, :, :]), bc[:, 2:3], None, ALU.mult)
            for n in range(NV):
                ve.wait_ge(high, n + 1)
                vh = k.va[:, n, :, 0, :]
                nc.vector.tensor_tensor(k.va[:, n, :, 1, :], ps[:, n % NB, :].rearrange("p (h d) -> p h d", h=H), vh,
                                        ALU.subtract).then_inc(low, 1)
            def rotated_low(j):
                b, t = (j // 2) % 2, j % 2
                if j // 2 >= 2:
                    ve.wait_ge(stored[b], 32 * (j // 4))
                ve.wait_ge(high, NV + j + 1)
                sl = slice((j % 2) * 1024, (j % 2 + 1) * 1024)
                nc.vector.tensor_tensor(ol[:, b, sl], t1[:, t, :], oh[:, b, sl], ALU.subtract).then_inc(low, 1)

            for j, (pr, i, half) in enumerate(pairs):
                if rotate:
                    t = j % 2
                    sl = slice(half * 1024, (half + 1) * 1024)
                    ve.wait_ge(job, NV + j + 1)
                    if j >= 2:
                        ve.wait_ge(low, NV + j - 1)
                    nc.vector.tensor_tensor(t1[:, t, :], ps[:, 2 * t, :], rope[:, 0, sl], ALU.mult).then_inc(prod, 1)
                    nc.vector.tensor_tensor(t2[:, t, :], ps[:, 2 * t + 1, :], rope[:, 1, sl], ALU.mult)\
                      .then_inc(prod, 1)
                    if j >= 1:
                        rotated_low(j - 1)
                    if j == len(pairs) - 1:
                        rotated_low(j)
                    continue
                n = NV + j
                b = (j // 2) % 2
                if j // 2 >= 2:
                    ve.wait_ge(stored[b], 32 * (j // 4))
                ve.wait_ge(high, n + 1)
                sl = slice(half * 1024, (half + 1) * 1024)
                nc.vector.tensor_tensor(ol[:, b, sl], ps[:, n % NB, :], oh[:, b, sl], ALU.subtract).then_inc(low, 1)

        @block.scalar
        def _(act):
            for n in range(NV):
                act.wait_ge(job, n + 1)
                nc.scalar.activation(k.va[:, n, :, 0, :], ps[:, n % NB, :].rearrange("p (h d) -> p h d", h=H),
                                     ACT.Copy).then_inc(high, 1)
            for j, (pr, i, half) in enumerate(pairs):
                n = NV + j
                b = (j // 2) % 2
                if j // 2 >= 2:
                    act.wait_ge(stored[b], 32 * (j // 4))
                if rotate:
                    act.wait_ge(rot, j + 1)
                    src = t1[:, j % 2, :]
                else:
                    act.wait_ge(job, n + 1)
                    src = ps[:, n % NB, :]
                nc.scalar.activation(oh[:, b, half * 1024:(half + 1) * 1024], src, ACT.Copy).then_inc(high, 1)

        if rotate:
            @block.gpsimd
            def _(pool):
                for j in range(len(pairs)):
                    pool.wait_ge(prod, 2 * j + 2)
                    nc.gpsimd.tensor_tensor(t1[:, j % 2, :], t1[:, j % 2, :], t2[:, j % 2, :], ALU.add)\
                      .then_inc(rot, 1)

        @block.tensor
        def _(pe):
            pe.wait_ge(scaled, 1)
            nc.tensor.transpose(ps[0:3, 0, 0:P], bc[:, :], k.ident[:, :]).then_inc(turned, 1)
            pe.wait_ge(scaled, 2)
            nc.tensor.matmul(ps[:, 1, 0:3], k.ones[0:3, 0:P], diag[:, :], start=True, stop=True).then_inc(peaked, 1)
            pe.wait_ge(wready, 1)
            for n in range(NV):
                if n >= NB:
                    pe.wait_ge(low, n - NB + 1)
                for c in range(2):
                    last = nc.tensor.matmul(ps[:, n % NB, c * 512:(c + 1) * 512], k.xnT[:, n * P:(n + 1) * P],
                                            w[:, 2, c * 512:(c + 1) * 512], start=True, stop=True)
                last.then_inc(job, 1)
            pe.wait_ge(wready, 5 if rotate else 3)
            for j, (pr, i, half) in enumerate(pairs):
                if rotate:
                    if j == 0:
                        pe.wait_ge(low, NV)
                    if j >= 2:
                        pe.wait_ge(prod, 2 * (j - 1))
                    for c in range(2):
                        q0 = half * 1024 + c * 512
                        for u, mat in enumerate((w, wsw)):
                            last = nc.tensor.matmul(ps[:, 2 * (j % 2) + u, c * 512:(c + 1) * 512],
                                                    mat[:, i, pr * P:(pr + 1) * P], k.xnT[:, q0:q0 + 512],
                                                    start=True, stop=True)
                    last.then_inc(job, 1)
                    continue
                n = NV + j
                pe.wait_ge(low, n - NB + 1)
                for c in range(2):
                    q0 = half * 1024 + c * 512
                    last = nc.tensor.matmul(ps[:, n % NB, c * 512:(c + 1) * 512], w[:, i, pr * P:(pr + 1) * P],
                                            k.xnT[:, q0:q0 + 512], start=True, stop=True)
                last.then_inc(job, 1)


def attention_stage(nc, k, layer, bias=False):
    with ExitStack() as ctx:
        m = Memory(nc, ctx)
        g = f"a{layer}_"
        qa = m.sb(g + "qa", [P, 2 * S], F16)
        ka = m.sb(g + "ka", [P, 2 * S], F16)
        qb = m.sb(g + "qb", [DH + 1, 2 * S], F16)
        kb = m.sb(g + "kb", [DH + 1, 2 * S], F16)
        room = [flat(k.xn[:, :, :]), k.xnT[:, :]]
        prob = [room[r // 2][:, (r % 2) * KP * QC:(r % 2 + 1) * KP * QC] for r in range(RING)]
        rem = m.sb(g + "rem", [P, RING, KP * QC], F16)
        osb, ssb = m.sb(g + "osb", [P, QC]), m.sb(g + "ssb", [P, QC])
        mx = m.sb(g + "mx", [P, 4, 4])
        m4 = m.sb(g + "m4", [P, 4])
        rs = m.sb(g + "rs", [P, 2, 2])
        st = m.ps(g + "st", [P, 2, QC])
        jb = m.ps(g + "jb", [P, 2, 512])
        xb = m.ps(g + "xb", [P, 2, 512])
        ov = m.ps(g + "ov", [P, QC])
        su = m.ps(g + "su", [P, QC])
        if bias:
            bh, bl = m.sb(g + "bh", [P, 2, BW], F16), m.sb(g + "bl", [P, 2, BW], F16)
            win = m.sb(g + "win", [P, 2, S])
            junk = m.sb(g + "junk", [P, 2, 512], BF16)
            beat = m.sb(g + "beat", [1, 2])
        ones_set = m.sem(g + "ones_set")
        loaded = m.sem(g + "loaded")
        max_ready, max_done = m.sem(g + "max_ready"), m.sem(g + "max_done")
        m4_done = m.sem(g + "m4_done")
        row_ready, row_done = m.sem(g + "row_ready"), m.sem(g + "row_done")
        st_ready, exp_done = m.sem(g + "st_ready"), m.sem(g + "exp_done")
        rem_vec, rem_pool = m.sem(g + "rem_vec"), m.sem(g + "rem_pool")
        pv_done = m.sem(g + "pv_done")
        ov_saved, su_saved = m.sem(g + "ov_saved"), m.sem(g + "su_saved")
        proj_ready, proj_done = m.sem(g + "proj_ready"), m.sem(g + "proj_done")
        rs_done = m.sem(g + "rs_done")
        win_done = m.sem(g + "win_done")
        loads = LOADS + (2 if bias else 0)
        block = ctx.enter_context(nc.Block())

        def cols(n):
            return (n % (2 * NC)) * QC

        def head(n):
            if isinstance(n, int):
                return n // NC
            return nc.s_assert_within(n >> (NC.bit_length() - 1), 0, H - 1,
                                      skip_runtime_bounds_check_because="chunks are numbered below heads * NC")

        def slot(n):
            return head(n) % 2

        def head_cols(n):
            return slot(n) * S

        def body(emit):
            emit.chunk(0, first=True)
            with emit.eng.Fori(1, NCH - AHEAD - 1) as n:
                emit.chunk(n)
            emit.chunk(NCH - AHEAD - 1, more=False)
            for n in range(NCH - AHEAD, NCH):
                emit.chunk(n, ahead=False, more=False)

        @block.sync
        def _(sp):
            def load(h, place):
                at = place * S
                for dst, which, store in ((qa[0:DH], 0, k.qk_high), (qa[DH:P], 0, k.qk_low), (qb[0:DH], 0, k.qk_high),
                                          (ka[0:DH], 1, k.qk_high), (ka[DH:P], 1, k.qk_high), (kb[0:DH], 1, k.qk_low)):
                    src = store[which].rearrange("a p s -> (a p) s")[bass.ds(h * DH, DH), :]
                    sp.dma_start(dst[:, bass.ds(at, S)], src).then_inc(loaded, 16)
                if bias:
                    for dst, part in ((bh, 0), (bl, 1)):
                        sp.dma_start(flat(dst[:, bass.ds(place, 1), :]), k.bias_rows(part, h)).then_inc(loaded, 16)

            load(0, 0)
            sp.wait_ge(loaded, 16 * loads)
            load(1, 1)
            with sp.Fori(2, H) as h:
                sp.wait_ge(loaded, 16 * loads * h)
                sp.wait_ge(st_ready, NC * NT * (h - 1))
                load(h, h % 2)

        class Tensor:
            eng = nc.tensor

            def maxima(self, m_, j):
                pe = nc.tensor
                if j >= 2 or not is_zero(m_):
                    pe.wait_ge(max_done, NJ * m_ + j - 1)
                if bias and j % 4 == 0:
                    pe.wait_ge(win_done, 4 * m_ + j // 4 + 1)
                apart(pe, ones_set)
                queries = qa[:, bass.ds(cols(m_) + (j // 4) * P, P)]
                nc.tensor.matmul(jb[:, j % 2, :], queries,
                                        ka[:, bass.ds(head_cols(m_) + (j % 4) * 512, 512)],
                                        start=True, stop=True).then_inc(max_ready, 1)

            def row(self, m_):
                pe = nc.tensor
                pe.wait_ge(m4_done, m_ + 1)
                for t in range(4):
                    last = nc.tensor.matmul(xb[0:1, 0, t * P:(t + 1) * P], m4[:, t:t + 1], k.ident[:, :],
                                            start=True, stop=True)
                last.then_inc(row_ready, 1)

            def value(self, n, s):
                pe = nc.tensor
                if s in POOL_RANK:
                    pe.wait_ge(rem_pool, len(POOL_STEPS) * n + POOL_RANK[s] + 1)
                else:
                    pe.wait_ge(rem_vec, len(VEC_STEPS) * n + VEC_RANK[s] + 1)
                if s == 0 and not is_zero(n):
                    pe.wait_ge(ov_saved, n)
                apart(pe, ones_set)
                r = s % RING
                high = prob[r].bitcast(BF16).rearrange("p (n t) -> p n t", t=2)[:, :, 1]
                parts = []
                for t in range(KP):
                    parts += [high[:, t * QC:(t + 1) * QC], rem[:, r, t * QC:(t + 1) * QC]]
                va = k.va[:, :, :, :, :].rearrange("p t h a d -> p t (h a d)")
                for i, moving in enumerate(parts):
                    t = KP * s + i // 2
                    nc.tensor.matmul(ov[:, :], va[:, t, bass.ds(head(n) * P, P)], moving,
                                     start=(s == 0 and i == 0), stop=(s == NS - 1 and i == 3))
                if s == 0 and not is_zero(n):
                    pe.wait_ge(su_saved, n)
                for i, moving in enumerate(parts):
                    last = nc.tensor.matmul(su[32 * i:32 * i + 32, :], k.ones32[:, :], moving,
                                            start=(s == 0), stop=(s == NS - 1))
                last.then_inc(pv_done, 1)

            def project(self, n, e):
                pe = nc.tensor
                if e == 0:
                    pe.wait_ge(su_saved, n + 1)
                wo = flat(k.wo[:, :, :])
                for t in range(2):
                    nc.tensor.matmul(xb[:, e, 2 * P + t:2 * P + t + 1], ssb[:, (2 * e + t) * P:(2 * e + t + 1) * P],
                                     k.ones[:, 0:1], start=(t == 0), stop=True, skip_group_check=True)
                for t in range(2):
                    last = nc.tensor.matmul(xb[:, e, t * P:(t + 1) * P], osb[:, (2 * e + t) * P:(2 * e + t + 1) * P],
                                            wo[:, bass.ds(head(n) * D, D)], start=False, stop=True,
                                            skip_group_check=True)
                last.then_inc(proj_ready, 1)

            def chunk(self, n, first=False, ahead=True, more=True):
                pe = nc.tensor
                pe.wait_ge(row_done, n + 1)
                if ahead:
                    pe.wait_ge(loaded, 16 * loads * (head(n + AHEAD) + 1))
                for s in range(NS):
                    for t in range(KP):
                        kt = KP * s + t
                        if not (first and kt < 2):
                            pe.wait_ge(exp_done, NT * n + kt - 1)
                        apart(pe, ones_set)
                        o = st[:, t, :]
                        nc.tensor.matmul(o, ka[:, bass.ds(head_cols(n) + kt * P, P)], qa[:, bass.ds(cols(n), QC)],
                                         start=True, stop=False)
                        if bias:
                            off = (n % NC) * QC - kt * P + (S - P)
                            for tab in (bh, bl):
                                nc.tensor.matmul(o, k.flipu[:, :],
                                                 flat(tab[:, :, :])[:, bass.ds(slot(n) * BW + off, QC)],
                                                 start=False, stop=False)
                        nc.tensor.matmul(o, kb[:, bass.ds(head_cols(n) + kt * P, P)], qb[:, bass.ds(cols(n), QC)],
                                         start=False, stop=True).then_inc(st_ready, 1)
                        if ahead and t == 0:
                            self.maxima(n + AHEAD, 2 * s)
                    if s == ROW_STEP and not (isinstance(n, int) and n == NCH - 1):
                        if not first:
                            pe.wait_ge(proj_done, 2 * (n - 1) + 1)
                        self.row(n + 1)
                    if s in OUT_STEPS and not first:
                        e = OUT_STEPS.index(s)
                        if e == 0 and not (isinstance(n, int) and n == NCH - 1):
                            pe.wait_ge(row_done, n + 2)
                        self.project(n - 1, e)
                    if s >= LAG:
                        self.value(n, s - LAG)
                    elif not first:
                        self.value(n - 1, NS + s - LAG)
                    if ahead:
                        self.maxima(n + AHEAD, 2 * s + 1)

        @block.tensor
        def _(pe):
            emit = Tensor()
            pe.wait_ge(ones_set, 1)
            pe.wait_ge(loaded, 16 * loads)
            for c in range(AHEAD):
                for j in range(NJ):
                    emit.maxima(c, j)
                if c == 0:
                    emit.row(0)
            body(emit)
            for s in range(NS - LAG, NS):
                emit.value(NCH - 1, s)
            pe.wait_ge(proj_done, 2 * (NCH - 1) + 1)
            for e in range(2):
                emit.project(NCH - 1, e)

        class Scalar:
            eng = nc.scalar

            def row(self, m_):
                act = nc.scalar
                act.wait_ge(row_ready, m_ + 1)
                apart(act, ones_set)
                nc.scalar.activation(qb[DH:DH + 1, bass.ds(cols(m_), QC)], xb[0:1, 0, :], ACT.Copy,
                                     scale=1.0 / MAXROW).then_inc(row_done, 1)

            def copy_out(self, n):
                act = nc.scalar
                act.wait_ge(pv_done, NS * (n + 1))
                if not is_zero(n):
                    act.wait_ge(proj_ready, 2 * n)
                nc.scalar.activation(osb[:, :], ov[:, :], ACT.Copy).then_inc(ov_saved, 1)
                nc.scalar.activation(ssb[:, :], su[:, :], ACT.Copy).then_inc(su_saved, 1)

            def window(self, m_, q):
                act = nc.scalar
                if q >= 2 or not is_zero(m_):
                    act.wait_ge(max_done, NJ * m_ + 4 * (q - 1))
                elif q == 0:
                    act.wait_ge(loaded, 16 * loads)
                apart(act, ones_set)
                off = (m_ % NC) * QC + q * P
                nc.scalar.activation(win[:, q % 2, ::-1], flat(bh[:, :, :])[:, bass.ds(slot(m_) * BW + off, S)], ACT.Copy,
                                     scale=k.unit[:, 0:1]).then_inc(win_done, 1)

            def chunk(self, n, first=False, ahead=True, more=True):
                act = nc.scalar
                for s in range(NS):
                    if s == ROW_STEP and not (isinstance(n, int) and n == NCH - 1):
                        self.row(n + 1)
                    if not (first and s < RING):
                        act.wait_ge(pv_done, NS * n + s - RING + 1)
                    for t in range(KP):
                        act.wait_ge(st_ready, NT * n + KP * s + t + 1)
                        nc.scalar.activation(prob[s % RING][:, t * QC:(t + 1) * QC], st[:, t, :], ACT.Exp,
                                             scale=k.sscale[:, 0:1]).then_inc(exp_done, 1)
                    if bias and ahead and s in (1, 3, 5):
                        self.window(n + AHEAD, (s + 1) // 2)
                    if bias and more and s == NS - 1:
                        act.wait_ge(loaded, 16 * loads * (head(n + AHEAD + 1) + 1))
                        self.window(n + AHEAD + 1, 0)
                    if s == LAG - 1 and not first:
                        self.copy_out(n - 1)

        @block.scalar
        def _(act):
            emit = Scalar()
            if bias:
                for c in range(AHEAD):
                    for q in range(4):
                        emit.window(c, q)
                    if c == 0:
                        emit.row(0)
                emit.window(AHEAD, 0)
            else:
                emit.row(0)
            body(emit)
            emit.copy_out(NCH - 1)

        class Vector:
            eng = nc.vector

            def maxima(self, m_, j):
                ve = nc.vector
                ve.wait_ge(max_ready, NJ * m_ + j + 1)
                out = mx[:, j // 4, j % 4:j % 4 + 1]
                if bias:
                    nc.vector.memset(beat[:, j % 2:j % 2 + 1], 0.0)
                    nc.vector.tensor_tensor_reduce(
                        out=junk[:, j % 2, :], in0=jb[:, j % 2, :], in1=win[:, (j // 4) % 2, (j % 4) * 512:(j % 4 + 1) * 512],
                        scale=1.0, scalar=-3.0e38, op0=ALU.add, op1=ALU.max, accum_out=out).then_inc(max_done, 1)
                else:
                    nc.vector.reduce_max(out, jb[:, j % 2, :], AX.X).then_inc(max_done, 1)

            def merge(self, m_):
                ve = nc.vector
                ve.wait_ge(max_done, NJ * m_ + NJ)
                if not is_zero(m_):
                    ve.wait_ge(row_ready, m_)
                nc.vector.tensor_reduce(m4[:, :], mx[:, :, :], AX.X, ALU.max).then_inc(m4_done, 1)
                ve.wait_ge(m4_done, m_ + 1)

            def accumulate(self, n, e):
                ve = nc.vector
                ve.wait_ge(proj_ready, 2 * n + e + 1)
                nc.vector.reciprocal(rs[:, e, :], xb[:, e, 2 * P:2 * P + 2]).then_inc(rs_done, 1)
                ve.wait_ge(rs_done, 2 * n + e + 1)
                apart(ve, ones_set)
                acc = flat(k.acc[:, :, :])
                for t in range(2):
                    a = acc[:, bass.ds((n % NC) * QC + (2 * e + t) * D, D)]
                    last = nc.vector.scalar_tensor_tensor(a, xb[:, e, t * P:(t + 1) * P], rs[:, e, t:t + 1], a,
                                                          ALU.mult, ALU.add)
                last.then_inc(proj_done, 1)

            def remainder(self, n, s, first):
                ve = nc.vector
                ve.wait_ge(exp_done, NT * n + KP * (s + 1))
                if not (first and s < RING):
                    ve.wait_ge(pv_done, NS * n + s - RING + 1)
                r = s % RING
                high = prob[r].bitcast(BF16).rearrange("p (n t) -> p n t", t=2)[:, :, 1]
                nc.vector.tensor_tensor(rem[:, r, :], prob[r], high, ALU.subtract).then_inc(rem_vec, 1)

            def chunk(self, n, first=False, ahead=True, more=True):
                for s in range(NS):
                    if s in OUT_STEPS and not first:
                        self.accumulate(n - 1, OUT_STEPS.index(s))
                    if ahead:
                        self.maxima(n + AHEAD, 2 * s)
                    if s - 1 in VEC_RANK:
                        self.remainder(n, s - 1, first)
                    if s == 0 and NS - 1 in VEC_RANK and not first:
                        self.remainder(n - 1, NS - 1, False)
                    if ahead:
                        self.maxima(n + AHEAD, 2 * s + 1)
                if ahead:
                    self.merge(n + AHEAD)

        @block.vector
        def _(ve):
            nc.vector.memset(kb[DH:DH + 1, :], -float(MAXROW)).then_inc(ones_set, 1)
            nc.vector.memset(flat(k.acc[:, :, :]), 0.0).then_inc(proj_done, 1)
            ve.wait_ge(proj_done, 1)
            emit = Vector()
            for c in range(AHEAD):
                for j in range(NJ):
                    emit.maxima(c, j)
                emit.merge(c)
            body(emit)
            if NS - 1 in VEC_RANK:
                emit.remainder(NCH - 1, NS - 1, False)
            for e in range(2):
                emit.accumulate(NCH - 1, e)

        class Pool:
            eng = nc.gpsimd

            def chunk(self, n, first=False, ahead=True, more=True):
                pool = nc.gpsimd
                for s in POOL_STEPS:
                    pool.wait_ge(exp_done, NT * n + KP * (s + 1))
                    if not (first and s < RING):
                        pool.wait_ge(pv_done, NS * n + s - RING + 1)
                    r = s % RING
                    high = prob[r].bitcast(BF16).rearrange("p (n t) -> p n t", t=2)[:, :, 1]
                    nc.gpsimd.tensor_tensor(rem[:, r, :], prob[r], high, ALU.subtract).then_inc(rem_pool, 1)

        @block.gpsimd
        def _(pool):
            body(Pool())


def combine_stage(nc, k, layer, gate, out=None):
    with ExitStack() as ctx:
        m = Memory(nc, ctx)
        prod, summed, stored = m.sem(f"m{layer}_prod"), m.sem(f"m{layer}_sum"), m.sem(f"m{layer}_stored")
        block = ctx.enter_context(nc.Block())

        @block.vector
        def _(ve):
            for t in range(NT):
                nc.vector.tensor_tensor(k.acc[:, t, :], k.acc[:, t, :], gate[:, t, :], ALU.mult).then_inc(prod, 1)
            for t in range(NT):
                ve.wait_ge(prod, t + 1)
                nc.vector.tensor_tensor(k.x[:, t, :], k.x[:, t, :], k.acc[:, t, :], ALU.add).then_inc(summed, 1)

        if out is not None:
            @block.sync
            def _(sp):
                o = out.rearrange("a (t p) m -> p (a t) m", p=P)
                for q in range(4):
                    sp.wait_ge(summed, 4 * q + 4)
                    sp.dma_start(o[:, 4 * q:4 * q + 4, :], k.x[:, 4 * q:4 * q + 4, :]).then_inc(stored, 16)
                sp.wait_ge(stored, 64)


def experts_stage(nc, k, t):
    with ExitStack() as outer:
        mo = Memory(nc, outer)
        nT = mo.sb("ex_nT", [D, S])
        onehot = mo.sb("ex_onehot", [P, NT, NE])
        oneT = mo.sb("ex_oneT", [NE, S])
        prob = mo.sb("ex_prob", [P, NT])
        router_stage(nc, k, t, onehot, oneT, prob)
        with ExitStack() as ctx:
            m = Memory(nc, ctx)
            gain, shift = m.sb("ex_gain", [P, D]), m.sb("ex_shift", [P, D])
            with ExitStack() as c2:
                loaded = Memory(nc, c2).sem("ex_affine")
                block = c2.enter_context(nc.Block())

                @block.sync
                def _(sp):
                    sp.dma_start(gain[:, :], t["L1_ffn_ln_g"].partition_broadcast(P)).then_inc(loaded, 16)
                    sp.dma_start(shift[:, :], t["L1_ffn_ln_b"].partition_broadcast(P)).then_inc(loaded, 16)
                    sp.wait_ge(loaded, 32)

            layernorm_stage(nc, k, "n2_", k.xn, k.acc, nT, affine=(gain[:, :], shift[:, :]))
        expert_products_stage(nc, k, t, nT, onehot, oneT, prob)


def router_stage(nc, k, t, onehot, oneT, prob):
    with ExitStack() as ctx:
        m = Memory(nc, ctx)
        wr, br = m.sb("rt_w", [D, NE]), m.sb("rt_b", [1, NE])
        logit, rank = m.sb("rt_logit", [P, NT, NE]), m.sb("rt_rank", [P, NT, NE])
        ranki = m.sb("rt_ranki", [P, NT, NE], mybir.dt.int32)
        e, top = m.sb("rt_e", [P, NT, NE]), m.sb("rt_top", [P, NT])
        ps = m.ps("rt_ps", [P, NT, NE])
        tp = m.ps("rt_tp", [NE, 4, 512])
        loaded, made, counted, chain = m.sem("rt_loaded"), m.sem("rt_made"), m.sem("rt_counted"), m.sem("rt_chain")
        shifted, exped, chosen, turned, copied = (m.sem("rt_shifted"), m.sem("rt_exped"), m.sem("rt_chosen"),
                                                  m.sem("rt_turned"), m.sem("rt_copied"))
        block = ctx.enter_context(nc.Block())

        @block.sync
        def _(sp):
            sp.dma_start(wr[:, :], t["L1_ffn_Wr"]).then_inc(loaded, 16)
            sp.dma_start(br[:, :], t["L1_ffn_br"].rearrange("(a e) -> a e", a=1)).then_inc(loaded, 16)

        @block.gpsimd
        def _(pool):
            nc.gpsimd.iota(ranki[:, :, :], pattern=[[0, NT], [-1, NE]], base=NE, channel_multiplier=0)\
              .then_inc(counted, 1)

        @block.tensor
        def _(pe):
            pe.wait_ge(loaded, 32)
            for q in range(NT):
                nc.tensor.matmul(ps[:, q, :], k.xnT[:, q * P:(q + 1) * P], wr[:, :], start=(q == 0), stop=False,
                                 skip_group_check=True)
                last = nc.tensor.matmul(ps[:, q, :], k.ones[0:1, 0:P], br[:, :], start=False, stop=True,
                                        skip_group_check=True)
            last.then_inc(made, 1)
            pe.wait_ge(chosen, 1)
            for q in range(NT):
                last = nc.tensor.transpose(tp[:, q // 4, (q % 4) * P:(q % 4 + 1) * P], onehot[:, q, :], k.ident[:, :])
            last.then_inc(turned, 1)

        @block.vector
        def _(ve):
            done = 0

            def link(ins):
                nonlocal done
                done += 1
                ins.then_inc(chain, 1)
                ve.wait_ge(chain, done)

            def over(ap):
                return ap.unsqueeze(2).broadcast_to([P, NT, NE])

            ve.wait_ge(made, 1)
            link(nc.vector.tensor_copy(logit[:, :, :], ps[:, :, :]))
            link(nc.vector.tensor_reduce(top[:, :], logit[:, :, :], AX.X, ALU.max))
            nc.vector.tensor_tensor(e[:, :, :], logit[:, :, :], over(top[:, :]), ALU.subtract).then_inc(shifted, 1)
            ve.wait_ge(counted, 1)
            link(nc.vector.tensor_copy(rank[:, :, :], ranki[:, :, :]))
            link(nc.vector.tensor_tensor(logit[:, :, :], logit[:, :, :], over(top[:, :]), ALU.is_ge))
            link(nc.vector.tensor_tensor(logit[:, :, :], logit[:, :, :], rank[:, :, :], ALU.mult))
            link(nc.vector.tensor_reduce(top[:, :], logit[:, :, :], AX.X, ALU.max))
            nc.vector.tensor_tensor(onehot[:, :, :], logit[:, :, :], over(top[:, :]), ALU.is_equal).then_inc(chosen, 1)
            ve.wait_ge(exped, 1)
            link(nc.vector.tensor_reduce(prob[:, :], e[:, :, :], AX.X, ALU.add))
            link(nc.vector.reciprocal(prob[:, :], prob[:, :]))

        @block.scalar
        def _(act):
            act.wait_ge(shifted, 1)
            nc.scalar.activation(e[:, :, :], e[:, :, :], ACT.Exp).then_inc(exped, 1)
            act.wait_ge(turned, 1)
            for c in range(4):
                nc.scalar.activation(oneT[:, c * 512:(c + 1) * 512], tp[:, c, :], ACT.Copy).then_inc(copied, 1)


def expert_products_stage(nc, k, t, nT, onehot, oneT, prob):
    with ExitStack() as ctx:
        m = Memory(nc, ctx)
        w1, w2 = m.sb("ep_w1", [D, NE, FF]), m.sb("ep_w2", [P, FT, NE, D])
        b1, b2 = m.sb("ep_b1", [NE, FF]), m.sb("ep_b2", [NE, D])
        pick = m.sb("ep_pick", [NE, NE, P])
        room = k.va[:, :, :, :, :].rearrange("p t h a d -> p (t h a d)").bitcast(F32)
        masked = room[:, 0:2 * NE * QC].rearrange("p (b e q) -> p b e q", b=2, e=NE)
        hT = room[:, 2 * NE * QC:2 * (NE + FT) * QC].rearrange("p (b j q) -> p b j q", b=2, j=FT)
        mk = m.ps("ep_mk", [P, 2, QC])
        up = m.ps("ep_up", [P, 2, QC])
        dn = m.ps("ep_dn", [P, 2, 512])
        bb = m.ps("ep_bb", [P, 512])
        loaded, picked, spread, maskd = m.sem("ep_loaded"), m.sem("ep_picked"), m.sem("ep_spread"), m.sem("ep_masked")
        up_done, relu_done, dn_done, sum_done = m.sem("ep_up"), m.sem("ep_relu"), m.sem("ep_dn"), m.sem("ep_sum")
        biased, chain, gated = m.sem("ep_biased"), m.sem("ep_chain"), m.sem("ep_gated")
        y = k.acc
        block = ctx.enter_context(nc.Block())

        @block.sync
        def _(sp):
            sp.dma_start(w1[:, :, :], t["L1_ffn_W1"].rearrange("e m f -> m e f")).then_inc(loaded, 16)
            sp.dma_start(b1[:, :], t["L1_ffn_b1"]).then_inc(loaded, 16)
            sp.dma_start(b2[:, :], t["L1_ffn_b2"]).then_inc(loaded, 16)
            for j in range(FT):
                sp.dma_start(w2[:, j, :, :], t["L1_ffn_W2"][:, j * P:(j + 1) * P, :].rearrange("e f d -> f e d"))\
                  .then_inc(loaded, 16)

        @block.tensor
        def _(pe):
            pe.wait_ge(picked, 1)

            def masks(c):
                for e in range(NE):
                    n = NE * c + e
                    if n >= 2:
                        pe.wait_ge(maskd, n - 1)
                    nc.tensor.matmul(mk[:, n % 2, :], pick[:, e, :], oneT[:, c * QC:(c + 1) * QC],
                                     start=True, stop=True).then_inc(spread, 1)

            masks(0)
            pe.wait_ge(loaded, 16 * (3 + FT))
            for c in range(NC):
                pe.wait_ge(maskd, NE * (c + 1))
                for j in range(FT):
                    n = FT * c + j
                    if n >= 2:
                        pe.wait_ge(relu_done, n - 1)
                    nc.tensor.matmul(up[:, n % 2, :], b1[:, j * P:(j + 1) * P], oneT[:, c * QC:(c + 1) * QC],
                                     start=True, stop=False)
                    for e in range(NE):
                        last = nc.tensor.matmul(up[:, n % 2, :], w1[:, e, j * P:(j + 1) * P], masked[:, c % 2, e, :],
                                                start=False, stop=(e == NE - 1))
                    last.then_inc(up_done, 1)
                if c + 1 < NC:
                    masks(c + 1)
                pe.wait_ge(relu_done, FT * (c + 1))
                for q in range(4):
                    n = 4 * c + q
                    if n >= 1:
                        pe.wait_ge(sum_done, n)
                    nc.tensor.matmul(bb[:, 0:D], oneT[:, n * P:(n + 1) * P], b2[:, :], start=True, stop=True)
                    for half in range(2):
                        for j in range(FT):
                            last = nc.tensor.matmul(
                                dn[:, half, :], hT[:, c % 2, j, q * P:(q + 1) * P],
                                w2[:, j, 4 * half:4 * half + 4, :].rearrange("p e d -> p (e d)"),
                                start=(j == 0), stop=(j == FT - 1))
                    last.then_inc(dn_done, 1)

        @block.vector
        def _(ve):
            nc.vector.tensor_copy(pick[:, :, :], k.ident[0:NE, 0:NE].unsqueeze(2).broadcast_to([NE, NE, P]))\
              .then_inc(picked, 1)

            def mask(c):
                for e in range(NE):
                    n = NE * c + e
                    ve.wait_ge(spread, n + 1)
                    nc.vector.tensor_tensor(masked[:, c % 2, e, :], mk[:, n % 2, :], nT[:, c * QC:(c + 1) * QC],
                                            ALU.mult).then_inc(maskd, 1)

            mask(0)
            done = 0
            for c in range(NC):
                if c + 1 < NC:
                    if c >= 1:
                        ve.wait_ge(up_done, FT * c)
                    mask(c + 1)
                for q in range(4):
                    n = 4 * c + q
                    ve.wait_ge(dn_done, n + 1)
                    nc.vector.tensor_copy(y[:, n, :], bb[:, 0:D]).then_inc(chain, 1)
                    done += 1
                    for e in range(NE):
                        ve.wait_ge(chain, done)
                        ins = nc.vector.scalar_tensor_tensor(
                            y[:, n, :], dn[:, e // 4, (e % 4) * D:(e % 4 + 1) * D], onehot[:, n, e:e + 1],
                            y[:, n, :], ALU.mult, ALU.add)
                        if e < NE - 1:
                            ins.then_inc(chain, 1)
                            done += 1
                        else:
                            ins.then_inc(sum_done, 1)

        @block.scalar
        def _(act):
            for c in range(NC):
                if c >= 2:
                    act.wait_ge(dn_done, 4 * (c - 1))
                for j in range(FT):
                    n = FT * c + j
                    act.wait_ge(up_done, n + 1)
                    nc.scalar.activation(hT[:, c % 2, j, :], up[:, n % 2, :], ACT.Relu).then_inc(relu_done, 1)
            for n in range(NT):
                act.wait_ge(sum_done, n + 1)
                nc.scalar.activation(k.gate[:, n, :], y[:, n, :], ACT.Silu, scale=prob[:, n:n + 1]).then_inc(gated, 1)


class Shared:
    pass


def build(nc, t, out):
    with ExitStack() as ctx:
        m = Memory(nc, ctx)
        k = Shared()
        k.x = m.sb("x", [P, NT, D])
        k.xn = m.sb("xn", [P, NT, D])
        k.xnT = m.sb("xnT", [D, S])
        k.acc = m.sb("acc", [P, NT, D])
        k.gate = m.sb("gate", [P, NT, D])
        k.va = m.sb("va", [P, NT, H, 2, DH], F16)
        k.wo = m.sb("wo", [P, H, D])
        k.sscale = m.sb("sscale", [P, 1])
        k.ident, k.flip = m.sb("ident", [P, P]), m.sb("flip", [P, P])
        k.ones, k.ones32 = m.sb("ones", [P, P]), m.sb("ones32", [P, 32], F16)
        k.qk_high = nc.dram_tensor("qk_high", (2, H // 2, P, S), F16, kind="Internal").ap()
        k.qk_low = nc.dram_tensor("qk_low", (2, H // 2, P, S), F16, kind="Internal").ap()

        k.unit, k.flipu = m.sb("unit", [P, 1]), m.sb("flipu", [P, P], BF16)
        k.bias_line = nc.dram_tensor("bias_line", (2, H, LINE), F16, kind="Internal").ap()

        def bias_rows(part, h):
            line = k.bias_line
            rows = bass.AP(line.tensor, part * H * LINE, [[LINE, H], [1, P], [1, BW]])
            return rows[bass.ds(h, 1)].rearrange("a p w -> (a p) w")

        k.bias_rows = bias_rows

        constants_stage(nc, k, t["L0_attn_x"])
        layernorm_stage(nc, k, "n0_", k.x, k.xn, k.xnT)
        ternary_ffn_stage(nc, k, t["L0_ffn_W1"], t["L0_ffn_b1"], t["L0_ffn_W2"], t["L0_ffn_b2"], k.gate)
        with nc.sbuf_tensor("w0", [P, 3, H * DH], F32) as w:
            load_weights_stage(nc, k, w, t["L0_attn_kernel"], t["L0_attn_WO"])
            qkv_stage(nc, k, 0, w, 1.0 / (DH * DH * H))
        attention_stage(nc, k, 0)
        combine_stage(nc, k, 0, k.gate)
        layernorm_stage(nc, k, "n1_", k.x, k.xn, k.xnT)
        experts_stage(nc, k, t)
        with nc.sbuf_tensor("w1", [P, 3, H * DH], F32) as w, nc.sbuf_tensor("rope", [P, 2, S], F32) as table:
            turn_weights_stage(nc, k, w, t["L1_attn_qkv_w"], t["L1_attn_out_w"])
            rope_stage(nc, k, table, t["L1_attn_rope_freqs"])
            qkv_stage(nc, k, 1, w, DH ** -0.5, rope=table)
        bias_stage(nc, k, t["L1_attn_bias_p"], t["L1_attn_bias_a"])
        attention_stage(nc, k, 1, bias=True)
        combine_stage(nc, k, 1, k.gate, out)


_INS = ['L0_attn_x', 'L0_attn_kernel', 'L0_attn_WO', 'L0_ffn_W1', 'L0_ffn_b1', 'L0_ffn_W2', 'L0_ffn_b2',
        'L1_attn_qkv_w', 'L1_attn_out_w', 'L1_attn_bias_p', 'L1_attn_bias_a', 'L1_attn_rope_freqs',
        'L1_ffn_Wr', 'L1_ffn_br', 'L1_ffn_ln_g', 'L1_ffn_ln_b', 'L1_ffn_W1', 'L1_ffn_b1', 'L1_ffn_W2', 'L1_ffn_b2']


def kernel(**inputs):
    import numpy as _np
    import concourse.bacc as _bacc
    from concourse import mybir as _mybir
    from concourse.bass_utils import run_bass_kernel_spmd as _run

    nc = _bacc.Bacc("TRN2", target_bir_lowering=False, num_devices=1)
    arrays, args = {}, {}
    for name in _INS:
        a = _np.ascontiguousarray(inputs[name])
        arrays[f"in_{name}"] = a
        args[name] = nc.dram_tensor(f"in_{name}", a.shape, _mybir.dt.from_np(a.dtype), kind="ExternalInput").ap()
    out = nc.dram_tensor("out_0", (1, S, D), F32, kind="ExternalOutput").ap()
    build(nc, args, out)
    r = _run(nc, [arrays], core_ids=[0])
    return r.results[0]["out_0"]
```

```python
import concourse.bass as bass
from concourse import mybir
from contextlib import ExitStack

F32 = mybir.dt.float32
F16 = mybir.dt.float16
BF16 = mybir.dt.bfloat16
ALU = mybir.AluOpType
ACT = mybir.ActivationFunctionType
AX = mybir.AxisListType

P = 128
D = 128
S = 2048
H = 16
DH = 64
NT = S // P
QC = 512
NC = S // QC
NCH = H * NC
KP = 2
NS = NT // KP
FF = 512
FT = FF // P
NE = 8
LN_EPS = 1e-05
PEAK_MIN = 1e-15
MAXROW = P
RING = 4
LAG = 3
ROUND = 12582912.0
LINE = 2 * S
BW = S - P + S - QC + QC
AHEAD = 2
NJ = 16
ROW_STEP, OUT_STEPS = 2, (4, 5)
POOL_STEPS = ((0, 1, 5), tuple(range(NS)))
WINS, WIN_LEAD = 4, 2
LOADS = 6


class Memory:

    def __init__(self, nc, ctx):
        self.nc, self.ctx = nc, ctx

    def sb(self, name, shape, dt=F32):
        return self.ctx.enter_context(self.nc.sbuf_tensor(name, shape, dt))

    def ps(self, name, shape, dt=F32):
        return self.ctx.enter_context(self.nc.psum_tensor(name, shape, dt))

    def sem(self, name):
        return self.ctx.enter_context(self.nc.semaphore(name))


def is_zero(n):
    return isinstance(n, int) and n == 0


def apart(eng, sem):
    eng.wait_ge(sem, 1)


def flat(ap):
    return ap.rearrange("p a b -> p (a b)")


def constants_stage(nc, k, x):
    with ExitStack() as ctx:
        m = Memory(nc, ctx)
        zeroed, made, loaded = m.sem("c_zeroed"), m.sem("c_made"), m.sem("c_loaded")
        block = ctx.enter_context(nc.Block())

        @block.sync
        def _(sp):
            sp.dma_start(k.x[:, :, :], x.rearrange("a (t p) m -> p (a t) m", p=P)).then_inc(loaded, 16)
            sp.wait_ge(loaded, 16)

        @block.gpsimd
        def _(pool):
            nc.gpsimd.memset(k.ident[:, :], 0.0).then_inc(zeroed, 1)
            nc.gpsimd.memset(k.ones[:, :], 1.0)
            nc.gpsimd.memset(k.ones32[:, :], 1.0 / 32)
            pool.wait_ge(zeroed, 1)
            nc.gpsimd.affine_select(out=k.ident[:, :], in_=k.ident[:, :], compare_op=ALU.not_equal, fill=1.0,
                                    base=0, pattern=[[-1, P]], channel_multiplier=1).then_inc(made, 1)
            pool.wait_ge(made, 1)
            nc.gpsimd.tensor_copy(k.ident16[:, :], k.ident[:, :])


def layernorm_stage(nc, k, tag, src, dst, dstT, affine=None):
    with ExitStack() as ctx:
        m = Memory(nc, ctx)
        stats, mv = m.sb(tag + "stats", [P, NT, 6]), m.sb(tag + "mv", [P, NT, 2])
        std, rstd = m.sb(tag + "std", [P, NT]), m.sb(tag + "rstd", [P, NT])
        tp = m.ps(tag + "tp", [P, 4, 4, P])
        stats_done, mv_done, var_done = m.sem(tag + "stats_done"), m.sem(tag + "mv_done"), m.sem(tag + "var_done")
        std_done, rstd_done, tile_done = m.sem(tag + "std_done"), m.sem(tag + "rstd_done"), m.sem(tag + "tile_done")
        turned, copied, scaled = m.sem(tag + "turned"), m.sem(tag + "copied"), m.sem(tag + "scaled")
        block = ctx.enter_context(nc.Block())

        @block.vector
        def _(ve):
            for t in range(NT):
                nc.vector.bn_stats(stats[:, t, :], src[:, t, :]).then_inc(stats_done, 1)
            for t in range(NT):
                ve.wait_ge(stats_done, t + 1)
                nc.vector.bn_aggr(mv[:, t, :], stats[:, t, :]).then_inc(mv_done, 1)
            ve.wait_ge(mv_done, NT)
            nc.vector.tensor_scalar(std[:, :], mv[:, :, 1], LN_EPS, None, ALU.add).then_inc(var_done, 1)
            ve.wait_ge(std_done, 1)
            nc.vector.reciprocal(rstd[:, :], std[:, :]).then_inc(rstd_done, 1)
            ve.wait_ge(rstd_done, 1)
            if affine is not None:
                ve.wait_ge(affine[2], 32)
            for t in range(NT):
                ins = nc.vector.tensor_scalar(dst[:, t, :], src[:, t, :], mv[:, t, 0:1], rstd[:, t:t + 1],
                                              ALU.subtract, ALU.mult)
                if affine is None:
                    ins.then_inc(tile_done, 1)
                else:
                    gain, shift, _ = affine
                    ins.then_inc(scaled, 1)
                    ve.wait_ge(scaled, 2 * t + 1)
                    nc.vector.tensor_tensor(dst[:, t, :], dst[:, t, :], gain, ALU.mult).then_inc(scaled, 1)
                    ve.wait_ge(scaled, 2 * t + 2)
                    nc.vector.tensor_tensor(dst[:, t, :], dst[:, t, :], shift, ALU.add).then_inc(tile_done, 1)

        @block.tensor
        def _(pe):
            for t in range(NT):
                pe.wait_ge(tile_done, t + 1)
                nc.tensor.transpose(tp[:, t // 4, t % 4, :], dst[:, t, :], k.ident[:, :]).then_inc(turned, 1)

        @block.scalar
        def _(act):
            act.wait_ge(var_done, 1)
            nc.scalar.activation(std[:, :], std[:, :], ACT.Sqrt).then_inc(std_done, 1)
            for g in range(4):
                act.wait_ge(turned, 4 * g + 4)
                nc.scalar.activation(dstT[:, 4 * g * P:4 * (g + 1) * P], flat(tp[:, g, :, :]), ACT.Copy)\
                   .then_inc(copied, 1)


def ternary_ffn_stage(nc, k, W1, b1, W2, b2, gate):
    with ExitStack() as ctx:
        m = Memory(nc, ctx)
        w = m.sb("tf_w", [P, 2, FF])
        mag = m.sb("tf_mag", [P, 2, FF])
        part, scale = m.sb("tf_part", [P, 2]), m.sb("tf_scale", [P, 2])
        above, below = m.sb("tf_above", [P, 2]), m.sb("tf_below", [P, 2])
        t = m.sb("tf_t", [P, 2, FF])
        wT = m.sb("tf_wT", [P, 2, FF])
        bias1, bias2 = m.sb("tf_b1", [P, FT]), m.sb("tf_b2", [1, D])
        hT = m.sb("tf_hT", [P, FT, S])
        ps = m.ps("tf_ps", [P, 8, 512])
        loaded, mags, summed, scaled = m.sem("tf_loaded"), m.sem("tf_mags"), m.sem("tf_summed"), m.sem("tf_scaled")
        chain, turned, copied = m.sem("tf_chain"), m.sem("tf_turned"), m.sem("tf_copied")
        up, act_done, down, gated = m.sem("tf_up"), m.sem("tf_act"), m.sem("tf_down"), m.sem("tf_gated")
        block = ctx.enter_context(nc.Block())

        @block.sync
        def _(sp):
            sp.dma_start(w[:, 0, :].rearrange("p (j m) -> p j m", m=D),
                         W1.rearrange("(j p) m -> p j m", p=P)).then_inc(loaded, 16)
            sp.dma_start(w[:, 1, :], W2).then_inc(loaded, 16)
            sp.dma_start(bias1[:, :], b1.rearrange("(j p) -> p j", p=P),
                         allow_slow_non_contiguous=True).then_inc(loaded, 16)
            sp.dma_start(bias2[:, :], b2.rearrange("(a d) -> a d", a=1)).then_inc(loaded, 16)

        @block.scalar
        def _(act):
            act.wait_ge(loaded, 64)
            for i in range(2):
                nc.scalar.activation(mag[:, i, :], w[:, i, :], ACT.Abs).then_inc(mags, 1)
            for i in range(2):
                act.wait_ge(turned, i + 1)
                nc.scalar.activation(wT[:, i, :], ps[:, 1 + i, :], ACT.Copy).then_inc(copied, 1)
            for j in range(FT):
                for c in range(NC):
                    n = NC * j + c
                    act.wait_ge(up, n + 1)
                    nc.scalar.activation(hT[:, j, c * QC:(c + 1) * QC], ps[:, n % 4, :], ACT.Gelu,
                                         bias=bias1[:, j:j + 1]).then_inc(act_done, 1)
            for g in range(NT // 4):
                act.wait_ge(down, g + 1)
                nc.scalar.activation(flat(gate[:, 4 * g:4 * g + 4, :]), ps[:, 4 + g, :], ACT.Silu).then_inc(gated, 1)

        @block.vector
        def _(ve):
            done = 0

            def link(ins):
                nonlocal done
                done += 1
                ins.then_inc(chain, 1)
                ve.wait_ge(chain, done)

            ve.wait_ge(mags, 2)
            for i in range(2):
                link(nc.vector.reduce_sum(part[:, i:i + 1], mag[:, i, :], AX.X))
            ve.wait_ge(summed, 1)
            link(nc.vector.tensor_scalar(scale[:, :], ps[:, 0, 0:2], 1.0 / (FF * D), 1e-08, ALU.mult, ALU.max))
            link(nc.vector.tensor_scalar(above[:, :], scale[:, :], 0.5, None, ALU.mult))
            link(nc.vector.tensor_scalar(below[:, :], scale[:, :], -0.5, None, ALU.mult))
            for i in range(2):
                link(nc.vector.tensor_scalar(t[:, i, :], w[:, i, :], below[:, i:i + 1], None, ALU.is_lt))
                link(nc.vector.scalar_tensor_tensor(t[:, i, :], w[:, i, :], above[:, i:i + 1], t[:, i, :],
                                                    ALU.is_gt, ALU.subtract))
                link(nc.vector.tensor_tensor(t[:, i, :], t[:, i, :], w[:, i, :], ALU.subtract))
                nc.vector.tensor_tensor(t[:, i, :], t[:, i, :], w[:, i, :], ALU.add).then_inc(scaled, 1)

        @block.tensor
        def _(pe):
            pe.wait_ge(chain, 2)
            nc.tensor.matmul(ps[:, 0, 0:2], k.ones[:, 0:P], part[:, :], start=True, stop=True).then_inc(summed, 1)
            for i in range(2):
                pe.wait_ge(scaled, i + 1)
                for j in range(FT):
                    last = nc.tensor.transpose(ps[:, 1 + i, j * P:(j + 1) * P], t[:, i, j * P:(j + 1) * P],
                                               k.ident[:, :])
                last.then_inc(turned, 1)
            pe.wait_ge(copied, 2)
            for j in range(FT):
                for c in range(NC):
                    n = NC * j + c
                    if n >= 4:
                        pe.wait_ge(act_done, n - 3)
                    nc.tensor.matmul(ps[:, n % 4, :], wT[:, 0, j * P:(j + 1) * P], k.xnT[:, c * QC:(c + 1) * QC],
                                     start=True, stop=True).then_inc(up, 1)
            pe.wait_ge(act_done, FT * NC)
            for q in range(NT):
                o = ps[:, 4 + q // 4, (q % 4) * P:(q % 4 + 1) * P]
                for j in range(FT):
                    nc.tensor.matmul(o, hT[:, j, q * P:(q + 1) * P], wT[:, 1, j * P:(j + 1) * P],
                                     start=(j == 0), stop=False)
                last = nc.tensor.matmul(o, k.ones[0:1, 0:P], bias2[:, :], start=False, stop=True)
                if q % 4 == 3:
                    last.then_inc(down, 1)


def peak_of_weights(nc, ve, link, w, n, hi, lo, amax):
    for i in range(n):
        link(nc.vector.reduce_max(hi[:, i:i + 1], w[:, i, :], AX.X))
        link(nc.vector.tensor_reduce(lo[:, i:i + 1], w[:, i, :], AX.X, ALU.min))
    link(nc.vector.scalar_tensor_tensor(amax[:, 0:n], lo[:, 0:n], -1.0, hi[:, 0:n], ALU.mult, ALU.max))


def start_weight_loads(nc, k, w, W, Wo, loaded):
    with nc.Block() as block:

        @block.sync
        def _(sp):
            for i in range(3):
                sp.dma_start(w[:, i, :].rearrange("p (h d) -> p h d", h=H),
                             W[i].rearrange("h m d -> m h d")).then_inc(loaded, 16)
            for half in range(2):
                sp.dma_start(k.wo[half * DH:(half + 1) * DH, :, :],
                             Wo[0].rearrange("(d h) m -> d h m", h=H)).then_inc(loaded, 16)


def turn_weights_stage(nc, k, w, Wqkv, Wo):
    with ExitStack() as ctx:
        m = Memory(nc, ctx)
        NW = 3 * H * DH // P
        raw = m.sb("tw_raw", [P, NW, D])
        out2 = m.sb("tw_out2", [P, H, 2, DH])
        ps = m.ps("tw_ps", [P, 8, 4, P])
        loaded, loaded_o, turned, copied = m.sem("tw_loaded"), m.sem("tw_loaded_o"), m.sem("tw_turned"), m.sem("tw_copied")
        NG = (NW + H) // 4
        block = ctx.enter_context(nc.Block())

        @block.sync
        def _(sp):
            sp.dma_start(raw[:, :, :], Wqkv.rearrange("(t p) m -> p t m", p=P)).then_inc(loaded, 16)
            for half in range(2):
                sp.dma_start(out2[:, :, half, :], Wo.rearrange("m (h d) -> m h d", h=H)).then_inc(loaded_o, 16)

        @block.tensor
        def _(pe):
            pe.wait_ge(loaded, 16)
            for g in range(NG):
                if g == NW // 4:
                    pe.wait_ge(loaded_o, 32)
                if g >= 8:
                    pe.wait_ge(copied, g - 7)
                for q in range(4):
                    t = 4 * g + q
                    src = raw[:, t, :] if t < NW else out2[:, t - NW, :, :].rearrange("p a d -> p (a d)")
                    last = nc.tensor.transpose(ps[:, g % 8, q, :], src, k.ident[:, :])
                last.then_inc(turned, 1)

        @block.scalar
        def _(act):
            for g in range(NG):
                act.wait_ge(turned, g + 1)
                n = 4 * g
                if n < NW:
                    i, at = n // 8, (n % 8) * P
                    dst = w[:, i, at:at + 4 * P]
                else:
                    dst = flat(k.wo[:, n - NW:n - NW + 4, :])
                nc.scalar.activation(dst, flat(ps[:, g % 8, :, :]), ACT.Copy).then_inc(copied, 1)


TWO_PI_PARTS = (6.28125, 2029.0 / 2**20, 2 * 3.141592653589793 - 6.28125 - 2029.0 / 2**20)
HALF_PI = 1.5707963267948966
PI_INSIDE = 3.1415925


def rope_stage(nc, k, table, freqs):
    with ExitStack() as ctx:
        m = Memory(nc, ctx)
        pos = m.sb("rp_pos", [P, S], mybir.dt.int32)
        ang, turns = m.sb("rp_ang", [P, S]), m.sb("rp_turns", [P, S])
        freq = m.sb("rp_freq", [P, 1])
        loaded, counted, chain, reduced, done_ = (m.sem("rp_loaded"), m.sem("rp_counted"), m.sem("rp_chain"),
                                                  m.sem("rp_reduced"), m.sem("rp_done"))
        block = ctx.enter_context(nc.Block())

        @block.sync
        def _(sp):
            for q in range(P // 32):
                sp.dma_start(freq[32 * q:32 * q + 32, :], freqs.rearrange("(d a) -> d a", a=1),
                             allow_slow_non_contiguous=True).then_inc(loaded, 16)

        @block.gpsimd
        def _(pool):
            nc.gpsimd.iota(pos[:, :], pattern=[[1, S]], base=0, channel_multiplier=0).then_inc(counted, 1)

        @block.vector
        def _(ve):
            done = 0

            def link(ins):
                nonlocal done
                done += 1
                ins.then_inc(chain, 1)
                ve.wait_ge(chain, done)

            ve.wait_ge(counted, 1)
            link(nc.vector.tensor_copy(ang[:, :], pos[:, :]))
            ve.wait_ge(loaded, 16 * (P // 32))
            link(nc.vector.tensor_scalar(ang[:, :], ang[:, :], freq[:, 0:1], None, ALU.mult))
            for i in range(2):
                quarter = 0.25 if i == 0 else 0.0
                r = table[:, i, :]
                link(nc.vector.tensor_scalar(turns[:, :], ang[:, :], 0.15915494309189535, quarter, ALU.mult, ALU.add))
                link(nc.vector.tensor_scalar(turns[:, :], turns[:, :], ROUND, ROUND, ALU.add, ALU.subtract))
                for j, part in enumerate(TWO_PI_PARTS):
                    link(nc.vector.scalar_tensor_tensor(r, turns[:, :], -part, ang[:, :] if j == 0 else r,
                                                        ALU.mult, ALU.add))
                if i == 0:
                    link(nc.vector.tensor_scalar(r, r, HALF_PI, None, ALU.add))
                nc.vector.tensor_scalar(r, r, PI_INSIDE, -PI_INSIDE, ALU.min, ALU.max).then_inc(reduced, 1)

        @block.scalar
        def _(act):
            for i in range(2):
                act.wait_ge(reduced, i + 1)
                nc.scalar.activation(table[:, i, :], table[:, i, :], ACT.Sin).then_inc(done_, 1)


def bias_stage(nc, k, bias_p, bias_a):
    with ExitStack() as ctx:
        m = Memory(nc, ctx)
        ints = m.sb("bs_ints", [H, LINE], mybir.dt.int32)
        dist = m.sb("bs_dist", [H, LINE])
        p, a, unit = m.sb("bs_p", [H, 1]), m.sb("bs_a", [H, 1]), m.sb("bs_unit", [H, 1])
        loaded, counted, chain, ready = m.sem("bs_loaded"), m.sem("bs_counted"), m.sem("bs_chain"), m.sem("bs_ready")
        logged, biased, stored = m.sem("bs_logged"), m.sem("bs_biased"), m.sem("bs_stored")
        block = ctx.enter_context(nc.Block())

        @block.sync
        def _(sp):
            sp.dma_start(p[:, :], bias_p.rearrange("h a b -> h (a b)"),
                         allow_slow_non_contiguous=True).then_inc(loaded, 16)
            sp.dma_start(a[:, :], bias_a.rearrange("h a b -> h (a b)"),
                         allow_slow_non_contiguous=True).then_inc(loaded, 16)
            sp.wait_ge(biased, 1)
            sp.dma_start(k.bias_line, dist[:, :]).then_inc(stored, 16)
            sp.wait_ge(stored, 16)

        @block.gpsimd
        def _(pool):
            nc.gpsimd.iota(ints[:, :], pattern=[[1, LINE]], base=-(S - 1), channel_multiplier=0).then_inc(counted, 1)

        @block.vector
        def _(ve):
            done = 0

            def link(ins):
                nonlocal done
                done += 1
                ins.then_inc(chain, 1)
                ve.wait_ge(chain, done)

            link(nc.vector.reciprocal(unit[:, :], k.sscale[0:H, :]))
            ve.wait_ge(loaded, 32)
            link(nc.vector.tensor_scalar(a[:, :], a[:, :], 0.01, None, ALU.max))
            link(nc.vector.tensor_scalar(p[:, :], p[:, :], 0.01, -1.0, ALU.max, ALU.mult))
            link(nc.vector.tensor_tensor(p[:, :], p[:, :], unit[:, :], ALU.mult))
            ve.wait_ge(counted, 1)
            nc.vector.tensor_copy(dist[:, :], ints[:, :]).then_inc(ready, 1)
            ve.wait_ge(logged, 2)
            nc.vector.tensor_scalar(dist[:, :], dist[:, :], p[:, 0:1], None, ALU.mult).then_inc(biased, 1)

        @block.scalar
        def _(act):
            act.wait_ge(ready, 1)
            nc.scalar.activation(dist[:, :], dist[:, :], ACT.Abs).then_inc(logged, 1)
            act.wait_ge(logged, 1)
            nc.scalar.activation(dist[:, :], dist[:, :], ACT.Ln, scale=a[:, 0:1], bias=k.ones[0:H, 0:1])\
               .then_inc(logged, 1)


def qkv_stage(nc, k, layer, w, softmax_scale, rope=None, weights=None):
    rotate = rope is not None
    with ExitStack() as ctx:
        m = Memory(nc, ctx)
        g = f"q{layer}_"
        wsw = m.sb(g + "wsw", [P, 2, H * DH]) if rotate else None
        hi, lo = m.sb(g + "hi", [P, 3]), m.sb(g + "lo", [P, 3])
        amax, peak = m.sb(g + "amax", [P, 3]), m.sb(g + "peak", [3, 1])
        diag, inv = m.sb(g + "diag", [3, 3]), m.sb(g + "inv", [P, 3])
        bc = m.sb(g + "bc", [P, 3])
        NB = 4
        ps = m.ps(g + "ps", [P, NB, 1024])
        oh, ol = m.sb(g + "oh", [P, 2, S], F16), m.sb(g + "ol", [P, 2, S], F16)
        t1 = m.sb(g + "t1", [P, 2, 1024]) if rotate else None
        t2 = m.sb(g + "t2", [P, 2, 1024]) if rotate else None
        chain, turned, peaked = m.sem(g + "chain"), m.sem(g + "turned"), m.sem(g + "peaked")
        job, high, low, stored = m.sem(g + "job"), m.sem(g + "high"), m.sem(g + "low"), [m.sem(g + "stored0"), m.sem(g + "stored1")]
        wready, scaled = m.sem(g + "wready"), m.sem(g + "scaled")
        prod, rot = m.sem(g + "prod"), m.sem(g + "rot")
        NV = NT
        pairs = [(pr, i, half) for pr in range(H // 2) for i in range(2) for half in range(2)]
        block = ctx.enter_context(nc.Block())

        @block.sync
        def _(sp):
            for n in range(2 * (H // 2)):
                pr, i = divmod(n, 2)
                sp.wait_ge(high, NV + 2 * n + 2)
                sp.wait_ge(low, NV + 2 * n + 2)
                sp.dma_start(k.qk_high[i, pr], oh[:, n % 2, :]).then_inc(stored[n % 2], 16)
                sp.dma_start(k.qk_low[i, pr], ol[:, n % 2, :]).then_inc(stored[n % 2], 16)
            for b in range(2):
                sp.wait_ge(stored[b], 32 * (H // 2))

        @block.vector
        def _(ve):
            done = 0

            def link(ins):
                nonlocal done
                done += 1
                ins.then_inc(chain, 1)
                ve.wait_ge(chain, done)

            if weights is not None:
                ve.wait_ge(*weights)
            peak_of_weights(nc, ve, link, w, 3, hi, lo, amax)
            nc.vector.tensor_copy(bc[:, :], amax[:, :]).then_inc(scaled, 1)
            ve.wait_ge(turned, 1)
            link(nc.vector.reduce_max(peak[:, :], ps[0:3, 0, 0:P], AX.X))
            link(nc.vector.tensor_scalar(peak[:, :], peak[:, :], PEAK_MIN, None, ALU.max))
            nc.vector.tensor_scalar(diag[:, :], k.ident[0:3, 0:3], peak[:, 0:1], None, ALU.mult).then_inc(scaled, 1)
            ve.wait_ge(peaked, 1)
            link(nc.vector.tensor_copy(bc[:, :], ps[:, 1, 0:3]))
            link(nc.vector.reciprocal(inv[:, :], bc[:, :]))
            link(nc.vector.tensor_tensor(k.sscale[:, 0:1], bc[:, 0:1], bc[:, 1:2], ALU.mult))
            link(nc.vector.tensor_scalar(k.sscale[:, 0:1], k.sscale[:, 0:1], softmax_scale, None, ALU.mult))
            for i in (2, 0, 1):
                nc.vector.tensor_scalar(w[:, i, :], w[:, i, :], inv[:, i:i + 1], None, ALU.mult).then_inc(wready, 1)
            if rotate:
                ve.wait_ge(wready, 3)
                wq = w[:, 0:2, :].rearrange("p i (h r d) -> p (i h) r d", h=H, r=2)
                wp = wsw[:, :, :].rearrange("p i (h r d) -> p (i h) r d", h=H, r=2)
                nc.vector.tensor_scalar(wp[:, :, 0, :], wq[:, :, 1, :], -1.0, None, ALU.mult).then_inc(wready, 1)
                nc.vector.tensor_copy(wp[:, :, 1, :], wq[:, :, 0, :]).then_inc(wready, 1)
            nc.vector.tensor_scalar(flat(k.wo[:, :, :]), flat(k.wo[:, :, :]), bc[:, 2:3], None, ALU.mult)
            for n in range(NV):
                ve.wait_ge(high, n + 1)
                vh = k.va[:, n, :, 0, :]
                nc.vector.tensor_tensor(k.va[:, n, :, 1, :], ps[:, n % NB, :].rearrange("p (h d) -> p h d", h=H), vh,
                                        ALU.subtract).then_inc(low, 1)
            def rotated_low(j):
                b, t = (j // 2) % 2, j % 2
                if j // 2 >= 2:
                    ve.wait_ge(stored[b], 32 * (j // 4))
                ve.wait_ge(high, NV + j + 1)
                sl = slice((j % 2) * 1024, (j % 2 + 1) * 1024)
                nc.vector.tensor_tensor(ol[:, b, sl], t1[:, t, :], oh[:, b, sl], ALU.subtract).then_inc(low, 1)

            for j, (pr, i, half) in enumerate(pairs):
                if rotate:
                    t = j % 2
                    sl = slice(half * 1024, (half + 1) * 1024)
                    ve.wait_ge(job, NV + j + 1)
                    if j >= 2:
                        ve.wait_ge(low, NV + j - 1)
                    nc.vector.tensor_tensor(t1[:, t, :], ps[:, 2 * t, :], rope[:, 0, sl], ALU.mult).then_inc(prod, 1)
                    nc.vector.tensor_tensor(t2[:, t, :], ps[:, 2 * t + 1, :], rope[:, 1, sl], ALU.mult)\
                      .then_inc(prod, 1)
                    if j >= 1:
                        rotated_low(j - 1)
                    if j == len(pairs) - 1:
                        rotated_low(j)
                    continue
                n = NV + j
                b = (j // 2) % 2
                if j // 2 >= 2:
                    ve.wait_ge(stored[b], 32 * (j // 4))
                ve.wait_ge(high, n + 1)
                sl = slice(half * 1024, (half + 1) * 1024)
                nc.vector.tensor_tensor(ol[:, b, sl], ps[:, n % NB, :], oh[:, b, sl], ALU.subtract).then_inc(low, 1)

        @block.scalar
        def _(act):
            for n in range(NV):
                act.wait_ge(job, n + 1)
                nc.scalar.activation(k.va[:, n, :, 0, :], ps[:, n % NB, :].rearrange("p (h d) -> p h d", h=H),
                                     ACT.Copy).then_inc(high, 1)
            for j, (pr, i, half) in enumerate(pairs):
                n = NV + j
                b = (j // 2) % 2
                if j // 2 >= 2:
                    act.wait_ge(stored[b], 32 * (j // 4))
                if rotate:
                    act.wait_ge(rot, j + 1)
                    src = t1[:, j % 2, :]
                else:
                    act.wait_ge(job, n + 1)
                    src = ps[:, n % NB, :]
                nc.scalar.activation(oh[:, b, half * 1024:(half + 1) * 1024], src, ACT.Copy).then_inc(high, 1)

        if rotate:
            @block.gpsimd
            def _(pool):
                for j in range(len(pairs)):
                    pool.wait_ge(prod, 2 * j + 2)
                    nc.gpsimd.tensor_tensor(t1[:, j % 2, :], t1[:, j % 2, :], t2[:, j % 2, :], ALU.add)\
                      .then_inc(rot, 1)

        @block.tensor
        def _(pe):
            pe.wait_ge(scaled, 1)
            nc.tensor.transpose(ps[0:3, 0, 0:P], bc[:, :], k.ident[:, :]).then_inc(turned, 1)
            pe.wait_ge(scaled, 2)
            nc.tensor.matmul(ps[:, 1, 0:3], k.ones[0:3, 0:P], diag[:, :], start=True, stop=True).then_inc(peaked, 1)
            pe.wait_ge(wready, 1)
            for n in range(NV):
                if n >= NB:
                    pe.wait_ge(low, n - NB + 1)
                for c in range(2):
                    last = nc.tensor.matmul(ps[:, n % NB, c * 512:(c + 1) * 512], k.xnT[:, n * P:(n + 1) * P],
                                            w[:, 2, c * 512:(c + 1) * 512], start=True, stop=True)
                last.then_inc(job, 1)
            pe.wait_ge(wready, 5 if rotate else 3)
            for j, (pr, i, half) in enumerate(pairs):
                if rotate:
                    if j == 0:
                        pe.wait_ge(low, NV)
                    if j >= 2:
                        pe.wait_ge(prod, 2 * (j - 1))
                    for c in range(2):
                        q0 = half * 1024 + c * 512
                        for u, mat in enumerate((w, wsw)):
                            last = nc.tensor.matmul(ps[:, 2 * (j % 2) + u, c * 512:(c + 1) * 512],
                                                    mat[:, i, pr * P:(pr + 1) * P], k.xnT[:, q0:q0 + 512],
                                                    start=True, stop=True)
                    last.then_inc(job, 1)
                    continue
                n = NV + j
                pe.wait_ge(low, n - NB + 1)
                for c in range(2):
                    q0 = half * 1024 + c * 512
                    last = nc.tensor.matmul(ps[:, n % NB, c * 512:(c + 1) * 512], w[:, i, pr * P:(pr + 1) * P],
                                            k.xnT[:, q0:q0 + 512], start=True, stop=True)
                last.then_inc(job, 1)


def attention_stage(nc, k, layer, bias=False):
    with ExitStack() as ctx:
        m = Memory(nc, ctx)
        g = f"a{layer}_"
        qa = m.sb(g + "qa", [P, 2 * S], F16)
        ka = m.sb(g + "ka", [P, 2 * S], F16)
        qb = m.sb(g + "qb", [DH + 1, 2 * S], F16)
        kb = m.sb(g + "kb", [DH + 1, 2 * S], F16)
        room = [flat(k.xn[:, :, :]), k.xnT[:, :]]
        prob = [room[r // 2][:, (r % 2) * KP * QC:(r % 2 + 1) * KP * QC] for r in range(RING)]
        rem = m.sb(g + "rem", [P, RING, KP * QC], F16)
        osb, ssb = m.sb(g + "osb", [P, QC]), m.sb(g + "ssb", [P, QC])
        mx = m.sb(g + "mx", [P, 4, 4])
        m4, m4h = m.sb(g + "m4", [P, 4]), m.sb(g + "m4h", [P, 4], F16)
        rs = m.sb(g + "rs", [P, 2, 2])
        st = m.ps(g + "st", [P, 2, QC])
        jb = m.ps(g + "jb", [P, 2, 512])
        xb = m.ps(g + "xb", [P, 2, 512])
        ov = m.ps(g + "ov", [P, QC])
        su = m.ps(g + "su", [P, QC])
        if bias:
            tab = m.sb(g + "tab", [P, 2 * BW])
            win = m.sb(g + "win", [P, WINS, 1024], BF16)
            junk = m.sb(g + "junk", [P, 2, 512], BF16)
            beat = m.sb(g + "beat", [1, 2])
        pool_steps = POOL_STEPS[layer]
        vec_steps = tuple(s for s in range(NS) if s not in pool_steps)
        ones_set = m.sem(g + "ones_set")
        loaded = m.sem(g + "loaded")
        max_ready, max_done = m.sem(g + "max_ready"), m.sem(g + "max_done")
        merged, m4_done = m.sem(g + "merged"), m.sem(g + "m4_done")
        row_ready, row_done = m.sem(g + "row_ready"), m.sem(g + "row_done")
        st_ready, exp_done = m.sem(g + "st_ready"), m.sem(g + "exp_done")
        rem_vec, rem_pool = m.sem(g + "rem_vec"), m.sem(g + "rem_pool")
        pv_done = m.sem(g + "pv_done")
        ov_saved, su_saved = m.sem(g + "ov_saved"), m.sem(g + "su_saved")
        proj_ready, proj_done = m.sem(g + "proj_ready"), m.sem(g + "proj_done")
        rs_done = m.sem(g + "rs_done")
        win_done = m.sem(g + "win_done")
        added = m.sem(g + "added")
        st_read = added if bias else exp_done
        loads = LOADS + (1 if bias else 0)
        block = ctx.enter_context(nc.Block())

        def cols(n):
            return (n % (2 * NC)) * QC

        def head(n):
            if isinstance(n, int):
                return n // NC
            return nc.s_assert_within(n >> (NC.bit_length() - 1), 0, H - 1,
                                      skip_runtime_bounds_check_because="chunks are numbered below heads * NC")

        def slot(n):
            return head(n) % 2

        def head_cols(n):
            return slot(n) * S

        def body(emit):
            emit.chunk(0, first=True)
            pairs = (NCH - AHEAD - 2) // 2
            with emit.eng.Fori(0, pairs) as i:
                emit.chunk(2 * i + 1)
                emit.chunk(2 * i + 2)
            for n in range(2 * pairs + 1, NCH):
                emit.chunk(n, ahead=(n < NCH - AHEAD), more=(n < NCH - AHEAD - 1))

        @block.sync
        def _(sp):
            def load(h, place):
                at = place * S
                for dst, which, store in ((qa[0:DH], 0, k.qk_high), (qa[DH:P], 0, k.qk_low), (qb[0:DH], 0, k.qk_high),
                                          (ka[0:DH], 1, k.qk_high), (ka[DH:P], 1, k.qk_high), (kb[0:DH], 1, k.qk_low)):
                    src = store[which].rearrange("a p s -> (a p) s")[bass.ds(h * DH, DH), :]
                    sp.dma_start(dst[:, bass.ds(at, S)], src).then_inc(loaded, 16)
                if bias:
                    sp.dma_start(tab[:, bass.ds(place * BW, BW)], k.bias_rows(h)).then_inc(loaded, 16)

            load(0, 0)
            sp.wait_ge(loaded, 16 * loads)
            load(1, 1)
            with sp.Fori(2, H) as h:
                sp.wait_ge(loaded, 16 * loads * h)
                sp.wait_ge(st_read, NC * NT * (h - 1))
                load(h, h % 2)

        class Tensor:
            eng = nc.tensor

            def maxima(self, m_, j):
                pe = nc.tensor
                if j >= 2 or not is_zero(m_):
                    pe.wait_ge(max_done, NJ * m_ + j - 1)
                if bias and j % 2 == 0:
                    pe.wait_ge(win_done, NS * m_ + j // 2 + 1)
                apart(pe, ones_set)
                queries = qa[:, bass.ds(cols(m_) + (j // 4) * P, P)]
                nc.tensor.matmul(jb[:, j % 2, :], queries,
                                        ka[:, bass.ds(head_cols(m_) + (j % 4) * 512, 512)],
                                        start=True, stop=True).then_inc(max_ready, 1)

            def row(self, m_):
                pe = nc.tensor
                pe.wait_ge(m4_done, m_ + 1)
                for t in range(4):
                    last = nc.tensor.matmul(xb[0:1, 0, t * P:(t + 1) * P], m4h[:, t:t + 1], k.ident16[:, :],
                                            start=True, stop=True)
                last.then_inc(row_ready, 1)

            def value(self, n, s, u):
                pe = nc.tensor
                if u == 1:
                    self.value_products(n, s, u)
                    return
                if s in pool_steps:
                    pe.wait_ge(rem_pool, len(pool_steps) * n + pool_steps.index(s) + 1)
                else:
                    pe.wait_ge(rem_vec, len(vec_steps) * n + vec_steps.index(s) + 1)
                if s == 0 and not is_zero(n):
                    pe.wait_ge(ov_saved, n)
                apart(pe, ones_set)
                self.value_products(n, s, u)

            def value_products(self, n, s, u):
                pe = nc.tensor
                r = s % RING
                high = prob[r].bitcast(BF16).rearrange("p (n t) -> p n t", t=2)[:, :, 1]
                parts = []
                for t in range(KP):
                    parts += [high[:, t * QC:(t + 1) * QC], rem[:, r, t * QC:(t + 1) * QC]]
                va = k.va[:, :, :, :, :].rearrange("p t h a d -> p t (h a d)")
                for i in (2 * u, 2 * u + 1):
                    nc.tensor.matmul(ov[:, :], va[:, KP * s + u, bass.ds(head(n) * P, P)], parts[i],
                                     start=(s == 0 and i == 0), stop=(s == NS - 1 and i == 3))
                if u == 0:
                    return
                if s == 0 and not is_zero(n):
                    pe.wait_ge(su_saved, n)
                for i, moving in enumerate(parts):
                    last = nc.tensor.matmul(su[32 * i:32 * i + 32, :], k.ones32[:, :], moving,
                                            start=(s == 0), stop=(s == NS - 1))
                last.then_inc(pv_done, 1)

            def project(self, n, e):
                pe = nc.tensor
                if e == 0:
                    pe.wait_ge(su_saved, n + 1)
                wo = flat(k.wo[:, :, :])
                for t in range(2):
                    nc.tensor.matmul(xb[:, e, 2 * P + t:2 * P + t + 1], ssb[:, (2 * e + t) * P:(2 * e + t + 1) * P],
                                     k.ones[:, 0:1], start=(t == 0), stop=True, skip_group_check=True)
                for t in range(2):
                    last = nc.tensor.matmul(xb[:, e, t * P:(t + 1) * P], osb[:, (2 * e + t) * P:(2 * e + t + 1) * P],
                                            wo[:, bass.ds(head(n) * D, D)], start=False, stop=True,
                                            skip_group_check=True)
                last.then_inc(proj_ready, 1)

            def chunk(self, n, first=False, ahead=True, more=True):
                pe = nc.tensor
                pe.wait_ge(row_done, n + 1)
                if ahead:
                    pe.wait_ge(loaded, 16 * loads * (head(n + AHEAD) + 1))
                for s in range(NS):
                    for t in range(KP):
                        kt = KP * s + t
                        if not (first and kt < 2):
                            pe.wait_ge(st_read, NT * n + kt - 1)
                        apart(pe, ones_set)
                        o = st[:, t, :]
                        nc.tensor.matmul(o, ka[:, bass.ds(head_cols(n) + kt * P, P)], qa[:, bass.ds(cols(n), QC)],
                                         start=True, stop=False)
                        nc.tensor.matmul(o, kb[:, bass.ds(head_cols(n) + kt * P, P)], qb[:, bass.ds(cols(n), QC)],
                                         start=False, stop=True).then_inc(st_ready, 1)
                        if ahead:
                            self.maxima(n + AHEAD, KP * s + t)
                        if t == 0 and s > LAG:
                            self.value(n, s - LAG, t)
                        elif t == 0 and s < LAG and not first:
                            self.value(n - 1, NS + s - LAG, t)
                    if s == ROW_STEP and not (isinstance(n, int) and n == NCH - 1):
                        if not first:
                            pe.wait_ge(proj_done, 2 * (n - 1) + 1)
                        self.row(n + 1)
                    if s in OUT_STEPS and not first:
                        e = OUT_STEPS.index(s)
                        if e == 0 and not (isinstance(n, int) and n == NCH - 1):
                            pe.wait_ge(row_done, n + 2)
                        self.project(n - 1, e)
                    if s == LAG:
                        self.value(n, 0, 0)
                    if s >= LAG:
                        self.value(n, s - LAG, 1)
                    elif not first:
                        self.value(n - 1, NS + s - LAG, 1)

        @block.tensor
        def _(pe):
            emit = Tensor()
            pe.wait_ge(ones_set, 1)
            pe.wait_ge(loaded, 16 * loads)
            for c in range(AHEAD):
                for j in range(NJ):
                    emit.maxima(c, j)
                if c == 0:
                    emit.row(0)
            body(emit)
            for s in range(NS - LAG, NS):
                for t in range(KP):
                    emit.value(NCH - 1, s, t)
            pe.wait_ge(proj_done, 2 * (NCH - 1) + 1)
            for e in range(2):
                emit.project(NCH - 1, e)

        class Scalar:
            eng = nc.scalar

            def row(self, m_):
                act = nc.scalar
                act.wait_ge(row_ready, m_ + 1)
                apart(act, ones_set)
                nc.scalar.activation(qb[DH:DH + 1, bass.ds(cols(m_), QC)], xb[0:1, 0, :], ACT.Copy)\
                   .then_inc(row_done, 1)

            def divide_maxima(self, m_):
                act = nc.scalar
                act.wait_ge(merged, m_ + 1)
                if not is_zero(m_):
                    act.wait_ge(row_ready, m_)
                nc.scalar.activation(m4h[:, :], m4[:, :], ACT.Copy, scale=1.0 / MAXROW).then_inc(m4_done, 1)

            def copy_out(self, n):
                act = nc.scalar
                act.wait_ge(pv_done, NS * (n + 1))
                if not is_zero(n):
                    act.wait_ge(proj_ready, 2 * n)
                nc.scalar.activation(osb[:, :], ov[:, :], ACT.Copy).then_inc(ov_saved, 1)
                nc.scalar.activation(ssb[:, :], su[:, :], ACT.Copy).then_inc(su_saved, 1)

            def window(self, m_, s):
                act = nc.scalar
                if s >= WINS or not is_zero(m_):
                    act.wait_ge(max_done, NJ * m_ + 2 * (s - WINS) + 2)
                elif s == 0:
                    act.wait_ge(loaded, 16 * loads)
                apart(act, ones_set)
                q, half = s // 2, s % 2
                off = (m_ % NC) * QC + q * P + (1 - half) * 1024
                nc.scalar.activation(win[:, s % WINS, ::-1], tab[:, bass.ds(slot(m_) * BW + off, 1024)], ACT.Copy)\
                   .then_inc(win_done, 1)

            def chunk(self, n, first=False, ahead=True, more=True):
                act = nc.scalar
                for s in range(NS):
                    if s == ROW_STEP - 1 and not (isinstance(n, int) and n == NCH - 1):
                        self.divide_maxima(n + 1)
                    if bias and s == ROW_STEP and not (isinstance(n, int) and n == NCH - 1):
                        self.row(n + 1)
                    if not bias and not (first and s < RING):
                        act.wait_ge(pv_done, NS * n + s - RING + 1)
                    for t in range(KP):
                        room_ = prob[s % RING][:, t * QC:(t + 1) * QC]
                        if bias:
                            act.wait_ge(added, NT * n + KP * s + t + 1)
                            nc.scalar.activation(room_, room_, ACT.Exp, scale=k.sscale[:, 0:1]).then_inc(exp_done, 1)
                            if t == 0 and s == LAG - 1 and not first:
                                self.copy_out(n - 1)
                        else:
                            act.wait_ge(st_ready, NT * n + KP * s + t + 1)
                            nc.scalar.activation(room_, st[:, t, :], ACT.Exp, scale=k.sscale[:, 0:1])\
                               .then_inc(exp_done, 1)
                    if not bias and s == ROW_STEP and not (isinstance(n, int) and n == NCH - 1):
                        self.row(n + 1)
                    if not bias and s == LAG - 1 and not first:
                        self.copy_out(n - 1)
                    if bias and ahead and s + WIN_LEAD < NS:
                        self.window(n + AHEAD, s + WIN_LEAD)
                    if bias and more and s + WIN_LEAD >= NS:
                        if s + WIN_LEAD == NS:
                            act.wait_ge(loaded, 16 * loads * (head(n + AHEAD + 1) + 1))
                        self.window(n + AHEAD + 1, s + WIN_LEAD - NS)

        @block.scalar
        def _(act):
            emit = Scalar()
            if bias:
                for c in range(AHEAD):
                    for s in range(NS):
                        emit.window(c, s)
                    if c == 0:
                        emit.divide_maxima(0)
                        emit.row(0)
                for s in range(WIN_LEAD):
                    emit.window(AHEAD, s)
            else:
                emit.divide_maxima(0)
                emit.row(0)
            body(emit)
            emit.copy_out(NCH - 1)

        class Vector:
            eng = nc.vector

            def maxima(self, m_, j):
                ve = nc.vector
                ve.wait_ge(max_ready, NJ * m_ + j + 1)
                out = mx[:, j // 4, j % 4:j % 4 + 1]
                if bias:
                    nc.vector.memset(beat[:, j % 2:j % 2 + 1], 0.0)
                    nc.vector.tensor_tensor_reduce(
                        out=junk[:, j % 2, :], in0=jb[:, j % 2, :], in1=win[:, (j // 2) % WINS, (j % 2) * 512:(j % 2 + 1) * 512],
                        scale=1.0, scalar=-3.0e38, op0=ALU.add, op1=ALU.max, accum_out=out).then_inc(max_done, 1)
                else:
                    nc.vector.reduce_max(out, jb[:, j % 2, :], AX.X).then_inc(max_done, 1)

            def merge(self, m_):
                ve = nc.vector
                ve.wait_ge(max_done, NJ * m_ + NJ)
                if not is_zero(m_):
                    ve.wait_ge(m4_done, m_)
                nc.vector.tensor_reduce(m4[:, :], mx[:, :, :], AX.X, ALU.max).then_inc(merged, 1)
                ve.wait_ge(merged, m_ + 1)

            def invert(self, n, e):
                ve = nc.vector
                ve.wait_ge(proj_ready, 2 * n + e + 1)
                nc.vector.reciprocal(rs[:, e, :], xb[:, e, 2 * P:2 * P + 2]).then_inc(rs_done, 1)

            def accumulate(self, n, e):
                ve = nc.vector
                ve.wait_ge(rs_done, 2 * n + e + 1)
                apart(ve, ones_set)
                acc = flat(k.acc[:, :, :])
                for t in range(2):
                    a = acc[:, bass.ds((n % NC) * QC + (2 * e + t) * D, D)]
                    last = nc.vector.scalar_tensor_tensor(a, xb[:, e, t * P:(t + 1) * P], rs[:, e, t:t + 1], a,
                                                          ALU.mult, ALU.add)
                last.then_inc(proj_done, 1)

            def add_bias(self, n, s, t, first):
                ve = nc.vector
                if t == 0 and not (first and s < RING):
                    ve.wait_ge(pv_done, NS * n + s - RING + 1)
                kt = KP * s + t
                ve.wait_ge(st_ready, NT * n + kt + 1)
                apart(ve, ones_set)
                window = tab[:, bass.ds(slot(n) * BW + S - QC + kt * P - (n % NC) * QC, QC)]
                nc.vector.tensor_tensor(prob[s % RING][:, t * QC:(t + 1) * QC][:, ::-1], st[:, t, ::-1], window, ALU.add)\
                  .then_inc(added, 1)

            def remainder(self, n, s, first):
                ve = nc.vector
                ve.wait_ge(exp_done, NT * n + KP * (s + 1))
                if not (first and s < RING):
                    ve.wait_ge(pv_done, NS * n + s - RING + 1)
                r = s % RING
                high = prob[r].bitcast(BF16).rearrange("p (n t) -> p n t", t=2)[:, :, 1]
                nc.vector.tensor_tensor(rem[:, r, :], prob[r], high, ALU.subtract).then_inc(rem_vec, 1)

            def chunk(self, n, first=False, ahead=True, more=True):
                for s in range(NS):
                    if bias:
                        self.add_bias(n, s, 0, first)
                    if s == 0 and (ahead or n == NCH - AHEAD):
                        self.merge(n - 1 + AHEAD)
                    if ahead:
                        self.maxima(n + AHEAD, 2 * s)
                    if bias:
                        self.add_bias(n, s, 1, first)
                    if s - 1 in vec_steps:
                        self.remainder(n, s - 1, first)
                    if s == 0 and NS - 1 in vec_steps and not first:
                        self.remainder(n - 1, NS - 1, False)
                    if s in OUT_STEPS and not first:
                        self.invert(n - 1, OUT_STEPS.index(s))
                    if ahead:
                        self.maxima(n + AHEAD, 2 * s + 1)
                    if s in OUT_STEPS and not first:
                        self.accumulate(n - 1, OUT_STEPS.index(s))

        @block.vector
        def _(ve):
            nc.vector.memset(kb[DH:DH + 1, :], -float(MAXROW)).then_inc(ones_set, 1)
            nc.vector.memset(flat(k.acc[:, :, :]), 0.0).then_inc(proj_done, 1)
            ve.wait_ge(proj_done, 1)
            emit = Vector()
            for c in range(AHEAD):
                for j in range(NJ):
                    emit.maxima(c, j)
                if c < AHEAD - 1:
                    emit.merge(c)
            body(emit)
            if NS - 1 in vec_steps:
                emit.remainder(NCH - 1, NS - 1, False)
            for e in range(2):
                emit.invert(NCH - 1, e)
                emit.accumulate(NCH - 1, e)

        class Pool:
            eng = nc.gpsimd

            def chunk(self, n, first=False, ahead=True, more=True):
                pool = nc.gpsimd
                for s in pool_steps:
                    pool.wait_ge(exp_done, NT * n + KP * (s + 1))
                    if not (first and s < RING):
                        pool.wait_ge(pv_done, NS * n + s - RING + 1)
                    r = s % RING
                    high = prob[r].bitcast(BF16).rearrange("p (n t) -> p n t", t=2)[:, :, 1]
                    nc.gpsimd.tensor_tensor(rem[:, r, :], prob[r], high, ALU.subtract).then_inc(rem_pool, 1)

        @block.gpsimd
        def _(pool):
            body(Pool())


def combine_stage(nc, k, layer, gate, out=None):
    with ExitStack() as ctx:
        m = Memory(nc, ctx)
        prod, summed, stored = m.sem(f"m{layer}_prod"), m.sem(f"m{layer}_sum"), m.sem(f"m{layer}_stored")
        block = ctx.enter_context(nc.Block())

        @block.vector
        def _(ve):
            for t in range(NT):
                nc.vector.tensor_tensor(k.acc[:, t, :], k.acc[:, t, :], gate[:, t, :], ALU.mult).then_inc(prod, 1)
            for t in range(NT):
                ve.wait_ge(prod, t + 1)
                nc.vector.tensor_tensor(k.x[:, t, :], k.x[:, t, :], k.acc[:, t, :], ALU.add).then_inc(summed, 1)

        if out is not None:
            @block.sync
            def _(sp):
                o = out.rearrange("a (t p) m -> p (a t) m", p=P)
                for q in range(4):
                    sp.wait_ge(summed, 4 * q + 4)
                    sp.dma_start(o[:, 4 * q:4 * q + 4, :], k.x[:, 4 * q:4 * q + 4, :]).then_inc(stored, 16)
                sp.wait_ge(stored, 64)


def experts_stage(nc, k, t):
    with ExitStack() as outer:
        mo = Memory(nc, outer)
        nT = mo.sb("ex_nT", [D, S])
        onehot = mo.sb("ex_onehot", [P, NT, NE])
        oneT, oneT16 = mo.sb("ex_oneT", [NE, S]), mo.sb("ex_oneT16", [NE, S], F16)
        prob = mo.sb("ex_prob", [P, NT])
        w1, w2 = mo.sb("ex_w1", [D, NE, FF]), mo.sb("ex_w2", [P, FT, NE, D])
        gain, shift = mo.sb("ex_gain", [P, D]), mo.sb("ex_shift", [P, D])
        affine_loaded, weights_loaded = mo.sem("ex_affine_loaded"), mo.sem("ex_weights_loaded")

        def start_loads(sp):
            sp.dma_start(gain[:, :], t["L1_ffn_ln_g"].partition_broadcast(P)).then_inc(affine_loaded, 16)
            sp.dma_start(shift[:, :], t["L1_ffn_ln_b"].partition_broadcast(P)).then_inc(affine_loaded, 16)
            sp.dma_start(w1[:, :, :], t["L1_ffn_W1"].rearrange("e m f -> m e f")).then_inc(weights_loaded, 16)
            for j in range(FT):
                sp.dma_start(w2[:, j, :, :], t["L1_ffn_W2"][:, j * P:(j + 1) * P, :].rearrange("e f d -> f e d"))\
                  .then_inc(weights_loaded, 16)

        router_stage(nc, k, t, onehot, oneT, oneT16, prob, start_loads)
        layernorm_stage(nc, k, "n2_", k.xn, k.acc, nT, affine=(gain[:, :], shift[:, :], affine_loaded))
        expert_products_stage(nc, k, t, nT, onehot, oneT, oneT16, prob, w1, w2, weights_loaded)


def router_stage(nc, k, t, onehot, oneT, oneT16, prob, start_loads):
    with ExitStack() as ctx:
        m = Memory(nc, ctx)
        wr, br = m.sb("rt_w", [D, NE]), m.sb("rt_b", [1, NE])
        logit, rank = m.sb("rt_logit", [P, NT, NE]), m.sb("rt_rank", [P, NT, NE])
        ranki = m.sb("rt_ranki", [P, NT, NE], mybir.dt.int32)
        e, top = m.sb("rt_e", [P, NT, NE]), m.sb("rt_top", [P, NT])
        ps = m.ps("rt_ps", [P, NT, NE])
        tp = m.ps("rt_tp", [NE, 4, 512])
        loaded, made, counted, chain = m.sem("rt_loaded"), m.sem("rt_made"), m.sem("rt_counted"), m.sem("rt_chain")
        shifted, exped, chosen, turned, copied = (m.sem("rt_shifted"), m.sem("rt_exped"), m.sem("rt_chosen"),
                                                  m.sem("rt_turned"), m.sem("rt_copied"))
        block = ctx.enter_context(nc.Block())

        @block.sync
        def _(sp):
            sp.dma_start(wr[:, :], t["L1_ffn_Wr"]).then_inc(loaded, 16)
            sp.dma_start(br[:, :], t["L1_ffn_br"].rearrange("(a e) -> a e", a=1)).then_inc(loaded, 16)
            start_loads(sp)

        @block.gpsimd
        def _(pool):
            nc.gpsimd.iota(ranki[:, :, :], pattern=[[0, NT], [-1, NE]], base=NE, channel_multiplier=0)\
              .then_inc(counted, 1)

        @block.tensor
        def _(pe):
            pe.wait_ge(loaded, 32)
            for q in range(NT):
                nc.tensor.matmul(ps[:, q, :], k.xnT[:, q * P:(q + 1) * P], wr[:, :], start=(q == 0), stop=False,
                                 skip_group_check=True)
                last = nc.tensor.matmul(ps[:, q, :], k.ones[0:1, 0:P], br[:, :], start=False, stop=True,
                                        skip_group_check=True)
            last.then_inc(made, 1)
            pe.wait_ge(chosen, 1)
            for q in range(NT):
                last = nc.tensor.transpose(tp[:, q // 4, (q % 4) * P:(q % 4 + 1) * P], onehot[:, q, :], k.ident[:, :])
            last.then_inc(turned, 1)

        @block.vector
        def _(ve):
            done = 0

            def link(ins):
                nonlocal done
                done += 1
                ins.then_inc(chain, 1)
                ve.wait_ge(chain, done)

            def over(ap):
                return ap.unsqueeze(2).broadcast_to([P, NT, NE])

            ve.wait_ge(made, 1)
            link(nc.vector.tensor_copy(logit[:, :, :], ps[:, :, :]))
            link(nc.vector.tensor_reduce(top[:, :], logit[:, :, :], AX.X, ALU.max))
            nc.vector.tensor_tensor(e[:, :, :], logit[:, :, :], over(top[:, :]), ALU.subtract).then_inc(shifted, 1)
            ve.wait_ge(counted, 1)
            link(nc.vector.tensor_copy(rank[:, :, :], ranki[:, :, :]))
            link(nc.vector.tensor_tensor(logit[:, :, :], logit[:, :, :], over(top[:, :]), ALU.is_ge))
            link(nc.vector.tensor_tensor(logit[:, :, :], logit[:, :, :], rank[:, :, :], ALU.mult))
            link(nc.vector.tensor_reduce(top[:, :], logit[:, :, :], AX.X, ALU.max))
            nc.vector.tensor_tensor(onehot[:, :, :], logit[:, :, :], over(top[:, :]), ALU.is_equal).then_inc(chosen, 1)
            ve.wait_ge(exped, 1)
            link(nc.vector.tensor_reduce(prob[:, :], e[:, :, :], AX.X, ALU.add))
            link(nc.vector.reciprocal(prob[:, :], prob[:, :]))

        @block.scalar
        def _(act):
            act.wait_ge(shifted, 1)
            nc.scalar.activation(e[:, :, :], e[:, :, :], ACT.Exp).then_inc(exped, 1)
            act.wait_ge(turned, 1)
            for c in range(4):
                nc.scalar.activation(oneT[:, c * 512:(c + 1) * 512], tp[:, c, :], ACT.Copy).then_inc(copied, 1)
                nc.scalar.activation(oneT16[:, c * 512:(c + 1) * 512], tp[:, c, :], ACT.Copy).then_inc(copied, 1)


def expert_products_stage(nc, k, t, nT, onehot, oneT, oneT16, prob, w1, w2, weights_loaded):
    with ExitStack() as ctx:
        m = Memory(nc, ctx)
        b1, b2 = m.sb("ep_b1", [NE, FF]), m.sb("ep_b2", [NE, D])
        pick = m.sb("ep_pick", [NE, NE, P], F16)
        room = k.va[:, :, :, :, :].rearrange("p t h a d -> p (t h a d)").bitcast(F32)
        masked = room[:, 0:2 * NE * QC].rearrange("p (b e q) -> p b e q", b=2, e=NE)
        hT = room[:, 2 * NE * QC:2 * (NE + FT) * QC].rearrange("p (b j q) -> p b j q", b=2, j=FT)
        mk = m.ps("ep_mk", [P, 2, QC])
        up = m.ps("ep_up", [P, 2, QC])
        dn = m.ps("ep_dn", [P, 2, 512])
        bb = m.ps("ep_bb", [P, 512])
        loaded, picked, spread, maskd = m.sem("ep_loaded"), m.sem("ep_picked"), m.sem("ep_spread"), m.sem("ep_masked")
        up_done, relu_done, dn_done, sum_done = m.sem("ep_up"), m.sem("ep_relu"), m.sem("ep_dn"), m.sem("ep_sum")
        biased, chain, gated = m.sem("ep_biased"), m.sem("ep_chain"), m.sem("ep_gated")
        y = k.acc
        block = ctx.enter_context(nc.Block())

        @block.sync
        def _(sp):
            sp.dma_start(b1[:, :], t["L1_ffn_b1"]).then_inc(loaded, 16)
            sp.dma_start(b2[:, :], t["L1_ffn_b2"]).then_inc(loaded, 16)

        @block.tensor
        def _(pe):
            pe.wait_ge(picked, 1)

            def masks(c):
                for e in range(NE):
                    n = NE * c + e
                    if n >= 2:
                        pe.wait_ge(maskd, n - 1)
                    nc.tensor.matmul(mk[:, n % 2, :], pick[:, e, :], oneT16[:, c * QC:(c + 1) * QC],
                                     start=True, stop=True).then_inc(spread, 1)

            masks(0)
            pe.wait_ge(loaded, 32)
            pe.wait_ge(weights_loaded, 16 * (1 + FT))
            for c in range(NC):
                pe.wait_ge(maskd, NE * (c + 1))
                for j in range(FT):
                    n = FT * c + j
                    if n >= 2:
                        pe.wait_ge(relu_done, n - 1)
                    nc.tensor.matmul(up[:, n % 2, :], b1[:, j * P:(j + 1) * P], oneT[:, c * QC:(c + 1) * QC],
                                     start=True, stop=False)
                    for e in range(NE):
                        last = nc.tensor.matmul(up[:, n % 2, :], w1[:, e, j * P:(j + 1) * P], masked[:, c % 2, e, :],
                                                start=False, stop=(e == NE - 1))
                    last.then_inc(up_done, 1)
                if c + 1 < NC:
                    masks(c + 1)
                pe.wait_ge(relu_done, FT * (c + 1))
                for q in range(4):
                    n = 4 * c + q
                    if n >= 1:
                        pe.wait_ge(sum_done, n)
                    nc.tensor.matmul(bb[:, 0:D], oneT[:, n * P:(n + 1) * P], b2[:, :], start=True, stop=True)
                    for half in range(2):
                        for j in range(FT):
                            last = nc.tensor.matmul(
                                dn[:, half, :], hT[:, c % 2, j, q * P:(q + 1) * P],
                                w2[:, j, 4 * half:4 * half + 4, :].rearrange("p e d -> p (e d)"),
                                start=(j == 0), stop=(j == FT - 1))
                    last.then_inc(dn_done, 1)

        @block.vector
        def _(ve):
            nc.vector.tensor_copy(pick[:, :, :], k.ident[0:NE, 0:NE].unsqueeze(2).broadcast_to([NE, NE, P]))\
              .then_inc(picked, 1)

            def mask(c):
                for e in range(NE):
                    n = NE * c + e
                    ve.wait_ge(spread, n + 1)
                    nc.vector.tensor_tensor(masked[:, c % 2, e, :], mk[:, n % 2, :], nT[:, c * QC:(c + 1) * QC],
                                            ALU.mult).then_inc(maskd, 1)

            mask(0)
            done = 0
            for c in range(NC):
                if c + 1 < NC:
                    if c >= 1:
                        ve.wait_ge(up_done, FT * c)
                    mask(c + 1)
                for q in range(4):
                    n = 4 * c + q
                    ve.wait_ge(dn_done, n + 1)
                    nc.vector.tensor_copy(y[:, n, :], bb[:, 0:D]).then_inc(chain, 1)
                    done += 1
                    for e in range(NE):
                        ve.wait_ge(chain, done)
                        ins = nc.vector.scalar_tensor_tensor(
                            y[:, n, :], dn[:, e // 4, (e % 4) * D:(e % 4 + 1) * D], onehot[:, n, e:e + 1],
                            y[:, n, :], ALU.mult, ALU.add)
                        if e < NE - 1:
                            ins.then_inc(chain, 1)
                            done += 1
                        else:
                            ins.then_inc(sum_done, 1)

        @block.scalar
        def _(act):
            for c in range(NC):
                if c >= 2:
                    act.wait_ge(dn_done, 4 * (c - 1))
                for j in range(FT):
                    n = FT * c + j
                    act.wait_ge(up_done, n + 1)
                    nc.scalar.activation(hT[:, c % 2, j, :], up[:, n % 2, :], ACT.Relu).then_inc(relu_done, 1)
            for n in range(NT):
                act.wait_ge(sum_done, n + 1)
                nc.scalar.activation(k.gate[:, n, :], y[:, n, :], ACT.Silu, scale=prob[:, n:n + 1]).then_inc(gated, 1)


class Shared:
    pass


def build(nc, t, out):
    with ExitStack() as ctx:
        m = Memory(nc, ctx)
        k = Shared()
        k.x = m.sb("x", [P, NT, D])
        k.xn = m.sb("xn", [P, NT, D])
        k.xnT = m.sb("xnT", [D, S])
        k.acc = m.sb("acc", [P, NT, D])
        k.gate = m.sb("gate", [P, NT, D])
        k.va = m.sb("va", [P, NT, H, 2, DH], F16)
        k.wo = m.sb("wo", [P, H, D])
        k.sscale = m.sb("sscale", [P, 1])
        k.ident, k.ident16 = m.sb("ident", [P, P]), m.sb("ident16", [P, P], F16)
        k.ones, k.ones32 = m.sb("ones", [P, P]), m.sb("ones32", [P, 32], F16)
        k.qk_high = nc.dram_tensor("qk_high", (2, H // 2, P, S), F16, kind="Internal").ap()
        k.qk_low = nc.dram_tensor("qk_low", (2, H // 2, P, S), F16, kind="Internal").ap()

        k.bias_line = nc.dram_tensor("bias_line", (H, LINE), F32, kind="Internal").ap()

        def bias_rows(h):
            rows = bass.AP(k.bias_line.tensor, 0, [[LINE, H], [1, P], [1, BW]])
            return rows[bass.ds(h, 1)].rearrange("a p w -> (a p) w")

        k.bias_rows = bias_rows

        with nc.sbuf_tensor("w0", [P, 3, H * DH], F32) as w, nc.semaphore("w0_loaded") as w_loaded:
            constants_stage(nc, k, t["L0_attn_x"])
            start_weight_loads(nc, k, w, t["L0_attn_kernel"], t["L0_attn_WO"], w_loaded)
            layernorm_stage(nc, k, "n0_", k.x, k.xn, k.xnT)
            ternary_ffn_stage(nc, k, t["L0_ffn_W1"], t["L0_ffn_b1"], t["L0_ffn_W2"], t["L0_ffn_b2"], k.gate)
            qkv_stage(nc, k, 0, w, 1.0 / (DH * DH * H), weights=(w_loaded, 80))
        attention_stage(nc, k, 0)
        combine_stage(nc, k, 0, k.gate)
        layernorm_stage(nc, k, "n1_", k.x, k.xn, k.xnT)
        experts_stage(nc, k, t)
        with nc.sbuf_tensor("w1", [P, 3, H * DH], F32) as w, nc.sbuf_tensor("rope", [P, 2, S], F32) as table:
            turn_weights_stage(nc, k, w, t["L1_attn_qkv_w"], t["L1_attn_out_w"])
            rope_stage(nc, k, table, t["L1_attn_rope_freqs"])
            qkv_stage(nc, k, 1, w, DH ** -0.5, rope=table)
        bias_stage(nc, k, t["L1_attn_bias_p"], t["L1_attn_bias_a"])
        attention_stage(nc, k, 1, bias=True)
        combine_stage(nc, k, 1, k.gate, out)


_INS = ['L0_attn_x', 'L0_attn_kernel', 'L0_attn_WO', 'L0_ffn_W1', 'L0_ffn_b1', 'L0_ffn_W2', 'L0_ffn_b2',
        'L1_attn_qkv_w', 'L1_attn_out_w', 'L1_attn_bias_p', 'L1_attn_bias_a', 'L1_attn_rope_freqs',
        'L1_ffn_Wr', 'L1_ffn_br', 'L1_ffn_ln_g', 'L1_ffn_ln_b', 'L1_ffn_W1', 'L1_ffn_b1', 'L1_ffn_W2', 'L1_ffn_b2']


def kernel(**inputs):
    import numpy as _np
    import concourse.bacc as _bacc
    from concourse import mybir as _mybir
    from concourse.bass_utils import run_bass_kernel_spmd as _run

    nc = _bacc.Bacc("TRN2", target_bir_lowering=False, num_devices=1)
    arrays, args = {}, {}
    for name in _INS:
        a = _np.ascontiguousarray(inputs[name])
        arrays[f"in_{name}"] = a
        args[name] = nc.dram_tensor(f"in_{name}", a.shape, _mybir.dt.from_np(a.dtype), kind="ExternalInput").ap()
    out = nc.dram_tensor("out_0", (1, S, D), F32, kind="ExternalOutput").ap()
    build(nc, args, out)
    r = _run(nc, [arrays], core_ids=[0])
    return r.results[0]["out_0"]
```
